# Optimizing a Trainium2 kernel written in Bass

```python
import numpy as np
import jax
import jax.numpy as jnp

def _softmax(x, axis=-1):
    return jax.nn.softmax(x, axis=axis)

def _gelu(x):
    return jax.nn.gelu(x, approximate=True)

def _silu(x):
    return jax.nn.silu(x)

def _sigmoid(x):
    return jax.nn.sigmoid(x)

def _layernorm(x, axis=-1, eps=1e-05):
    m = jnp.mean(x, axis=axis, keepdims=True)
    v = jnp.var(x, axis=axis, keepdims=True)
    return (x - m) / jnp.sqrt(v + eps)

def _scatter_add(tgt, idx, src, axis=0):
    return tgt.at[idx].add(src)

def _segment_sum(src, seg, n):
    return jax.ops.segment_sum(src, seg, n)
kernel_name = 'mk_flamingo_gated_d1_seqx_r8_426a03'

def setup_inputs(seed: int=0):
    np.random.seed(seed)
    _w = jnp.asarray

    def _rec_inputs():
        import jax
        import jax.numpy as jnp
        _rk = jax.random.key(seed)
        x = -0.0002928 + 1 * jax.random.normal(jax.random.fold_in(_rk, 1), (8, 128, 128), jnp.float32)
        _lenS = 128 - jax.random.randint(jax.random.fold_in(_rk, 7), (8,), 0, max(1, 128 // 4) + 1, jnp.int32)
        _lenS2 = 128 - jax.random.randint(jax.random.fold_in(_rk, 8), (8,), 0, max(1, 128 // 4) + 1, jnp.int32)
        _ctx_1024P = jax.random.normal(jax.random.fold_in(_rk, 11), (8, 16, 128), jnp.float32)
        _ctx_1024c = jax.random.dirichlet(jax.random.fold_in(_rk, 511), 0.3 * jnp.ones((16,), jnp.float32), (8, 128))
        _ctx_1024t = jnp.einsum('bsk,bkd->bsd', _ctx_1024c, _ctx_1024P)
        _ctx_1024t = _ctx_1024t * jax.lax.rsqrt(jnp.mean(jnp.square(_ctx_1024t)) + 1e-12) * 0.953939
        ctx_1024 = -1.39393e-06 + 0.999914 * (_ctx_1024t + 0.3 * jax.random.normal(jax.random.fold_in(_rk, 611), (8, 128, 128), jnp.float32))
        fside_Bx1xSxS2_0 = -4.48278e-06 + 1.00019 * jax.random.normal(jax.random.fold_in(_rk, 12), (8, 1, 128, 128), jnp.float32)
        _g = jax.random.normal(jax.random.fold_in(_rk, 9001), (2, 1), jnp.float32)
        _g = jnp.sign(_g) * jnp.maximum(jnp.abs(_g), 1.0) + (_g == 0) * 1.0
        g_xattn = _g[0]
        g_ffn = _g[1]
        return (x, ctx_1024, fside_Bx1xSxS2_0, g_xattn, g_ffn)
    x, ctx_1024, fside_Bx1xSxS2_0, g_xattn, g_ffn = _rec_inputs()

    def _L0_xattn_setup():
        import jax, jax.numpy as jnp
        import numpy as np
        B, S, D_FF = (2, 256, 128)
        NUM_HEADS, D_KV = (16, 64)
        INNER = NUM_HEADS * D_KV
        key = jax.random.key(seed)
        ks = jax.random.split(key, 8)
        scale = 1.0 / np.sqrt(D_FF)
        return {'q': jax.random.normal(ks[0], (B, S, D_FF), jnp.float32), 'k': jax.random.normal(ks[1], (B, S, D_FF), jnp.float32), 'v': jax.random.normal(ks[2], (B, S, D_FF), jnp.float32), 'attn_mask': jax.random.normal(ks[3], (B, 1, S, S), jnp.float32), 'Wq': jax.random.normal(ks[4], (INNER, D_FF), jnp.float32) * scale, 'Wk': jax.random.normal(ks[5], (INNER, D_FF), jnp.float32) * scale, 'Wv': jax.random.normal(ks[6], (INNER, D_FF), jnp.float32) * scale, 'Wo': jax.random.normal(ks[7], (D_FF, INNER), jnp.float32) * scale, 'num_heads': NUM_HEADS}
    _L0_xattn_all = _L0_xattn_setup()
    _L0_xattn_in = {k: v for k, v in _L0_xattn_all.items() if k in ('Wq', 'Wk', 'Wv', 'Wo')}
    del _L0_xattn_all

    def _L0_ffn_setup():
        import jax, jax.numpy as jnp
        import numpy as np
        B, S, H = (2, 256, 128)
        E_ROUTED = 8
        TOP_K = 2
        I = 256
        key = jax.random.key(seed)
        ks = jax.random.split(key, 9)
        s = 0.02
        return {'x': jax.random.normal(ks[0], (B, S, H), dtype=jnp.float32), 'shared_gate': jax.random.normal(ks[1], (I, H), dtype=jnp.float32) * s, 'shared_up': jax.random.normal(ks[2], (I, H), dtype=jnp.float32) * s, 'shared_down': jax.random.normal(ks[3], (H, I), dtype=jnp.float32) * s, 'gate_w': jax.random.normal(ks[4], (E_ROUTED, H, I), dtype=jnp.float32) * s, 'up_w': jax.random.normal(ks[5], (E_ROUTED, H, I), dtype=jnp.float32) * s, 'down_w': jax.random.normal(ks[6], (E_ROUTED, I, H), dtype=jnp.float32) * s, 'router_w': jax.random.normal(ks[7], (E_ROUTED, H), dtype=jnp.float32) * s, 'routing_bias': jnp.zeros((E_ROUTED,), dtype=jnp.float32)}
    _L0_ffn_all = _L0_ffn_setup()
    _L0_ffn_in = {k: v for k, v in _L0_ffn_all.items() if k in ('shared_gate', 'shared_up', 'shared_down', 'gate_w', 'up_w', 'down_w', 'router_w', 'routing_bias')}
    del _L0_ffn_all
    return {'x': x, 'ctx_1024': ctx_1024, 'fside_Bx1xSxS2_0': fside_Bx1xSxS2_0, 'g_xattn': g_xattn, 'g_ffn': g_ffn, 'L0_xattn_Wq': _L0_xattn_in['Wq'], 'L0_xattn_Wk': _L0_xattn_in['Wk'], 'L0_xattn_Wv': _L0_xattn_in['Wv'], 'L0_xattn_Wo': _L0_xattn_in['Wo'], 'L0_ffn_shared_gate': _L0_ffn_in['shared_gate'], 'L0_ffn_shared_up': _L0_ffn_in['shared_up'], 'L0_ffn_shared_down': _L0_ffn_in['shared_down'], 'L0_ffn_gate_w': _L0_ffn_in['gate_w'], 'L0_ffn_up_w': _L0_ffn_in['up_w'], 'L0_ffn_down_w': _L0_ffn_in['down_w'], 'L0_ffn_router_w': _L0_ffn_in['router_w'], 'L0_ffn_routing_bias': _L0_ffn_in['routing_bias']}

def reference(x, ctx_1024, fside_Bx1xSxS2_0, g_xattn, g_ffn, L0_xattn_Wq, L0_xattn_Wk, L0_xattn_Wv, L0_xattn_Wo, L0_ffn_shared_gate, L0_ffn_shared_up, L0_ffn_shared_down, L0_ffn_gate_w, L0_ffn_up_w, L0_ffn_down_w, L0_ffn_router_w, L0_ffn_routing_bias):
    import jax
    import jax.numpy as jnp

    def _L0_xattn_ref(q, k, v, attn_mask, Wq, Wk, Wv, Wo, num_heads):
        import jax, jax.numpy as jnp
        import numpy as np
        B, S, D_FF = (2, 256, 128)
        NUM_HEADS, D_KV = (16, 64)
        INNER = NUM_HEADS * D_KV
        b, s, _ = q.shape

        def proj_heads(x, W):
            y = jnp.einsum('bsd,ed->bse', x, W)
            return y.reshape(b, s, num_heads, -1).transpose(0, 2, 1, 3)
        qh = proj_heads(q, Wq)
        kh = proj_heads(k, Wk)
        vh = proj_heads(v, Wv)
        scores = jnp.einsum('bhqd,bhkd->bhqk', qh, kh) + attn_mask
        probs = jax.nn.softmax(scores, axis=-1)
        ctx = jnp.einsum('bhqk,bhkd->bhqd', probs, vh)
        ctx = ctx.transpose(0, 2, 1, 3).reshape(b, s, -1)
        return jnp.einsum('bse,de->bsd', ctx, Wo)

    def _L0_ffn_ref(x, shared_gate, shared_up, shared_down, gate_w, up_w, down_w, router_w, routing_bias):
        import jax, jax.numpy as jnp
        import numpy as np
        B, S, H = (2, 256, 128)
        E_ROUTED = 8
        TOP_K = 2
        I = 256
        b, s, h = x.shape
        shared = jnp.einsum('bsi,hi->bsh', jax.nn.silu(jnp.einsum('bsh,ih->bsi', x, shared_gate)) * jnp.einsum('bsh,ih->bsi', x, shared_up), shared_down)
        logits = jnp.einsum('bsh,eh->bse', x, router_w) + routing_bias
        probs = jax.nn.sigmoid(logits)
        scores, indices = jax.lax.top_k(probs, TOP_K)
        scores = scores / jnp.sum(scores, axis=-1, keepdims=True)
        t = b * s
        xf = x.reshape(t, h)
        idx = indices.reshape(t, TOP_K)
        sc = scores.reshape(t, TOP_K)
        w = jnp.zeros((t, E_ROUTED), dtype=x.dtype)
        w = w.at[jnp.arange(t)[:, None], idx].add(sc)
        g = jax.nn.silu(jnp.einsum('th,ehi->tei', xf, gate_w))
        u = jnp.einsum('th,ehi->tei', xf, up_w)
        combined = jnp.einsum('tei,eih,te->th', g * u, down_w, w)
        return shared + combined.reshape(b, s, h)
    x = x + jnp.tanh(g_xattn[0]) * _L0_xattn_ref(_layernorm(x, axis=-1), ctx_1024, ctx_1024, fside_Bx1xSxS2_0, L0_xattn_Wq, L0_xattn_Wk, L0_xattn_Wv, L0_xattn_Wo, 16)
    x = x + jnp.tanh(g_ffn[0]) * _L0_ffn_ref(_layernorm(x, axis=-1), L0_ffn_shared_gate, L0_ffn_shared_up, L0_ffn_shared_down, L0_ffn_gate_w, L0_ffn_up_w, L0_ffn_down_w, L0_ffn_router_w, L0_ffn_routing_bias)
    return x

_drawn_inputs = setup_inputs


def setup_inputs(seed=0):
    import zlib

    import numpy as np

    out = dict(_drawn_inputs(seed))
    spreads = {'L0_ffn_routing_bias': (0.0, 0.8)}
    factors = {'L0_ffn_shared_gate': 8.0,
     'L0_ffn_shared_up': 8.0,
     'L0_ffn_shared_down': 8.0,
     'L0_ffn_gate_w': 8.0,
     'L0_ffn_up_w': 8.0,
     'L0_ffn_down_w': 8.0,
     'L0_ffn_router_w': 8.0}
    for name, (base, spread) in spreads.items():
        noise = np.random.default_rng([zlib.crc32(name.encode()), seed]).standard_normal(out[name].shape)
        drawn = base * np.exp(spread * noise) if base else spread * noise
        out[name] = jnp.asarray(drawn.astype(out[name].dtype))
    for name, factor in factors.items():
        out[name] = (out[name] * factor).astype(out[name].dtype)
    return out
```

```python
from contextlib import ExitStack
from itertools import islice

import concourse.bass as bass
from concourse import mybir

ALU = mybir.AluOpType
ACT = mybir.ActivationFunctionType
F32 = mybir.dt.float32
F32R = mybir.dt.float32r
I32 = mybir.dt.int32
AX = mybir.AxisListType.X

P = 128
B = 8
HEADS = 16
DK = 64
INNER = HEADS * DK
CHUNKS = INNER // P
PAIRS = B // 2
GROUPS = 2 * B
E_ROUTED = 8
EXPERTS = E_ROUTED + 1
I_FFN = 256
EPS = 1e-5
HUGE = 3.0e38

PROJ_USES = 6
XT_USES = 2
LN2_STEPS = 10
SEED = float(0x5EF759DF - (1 << 30))
NEWTON = 3
WARM_UP = 3


def build(nc, x, ctxT, mask, wqT, wkT, wvT, woT, gu, down, routerT, rows, ident, out):
    with ExitStack() as stack:
        def sb(name, shape, dt=F32):
            return stack.enter_context(nc.sbuf_tensor(name, shape, dt))

        def bank(name):
            return stack.enter_context(nc.psum_tensor(name, [P, 512], F32))

        def sem(name):
            return stack.enter_context(nc.semaphore(name))

        ident_sb = sb("ident_sb", [P, P])
        rows_sb = sb("rows_sb", [P, 2 * E_ROUTED + 2])
        gates, bias_sb, iota_sb = rows_sb[:, 0:2], rows_sb[:, 2:2 + E_ROUTED], rows_sb[:, 2 + E_ROUTED:]
        tanh_g = sb("tanh_g", [P, 2])
        w_raw = {n: sb(f"w{n}_raw", [P, INNER]) for n in "qkv"}
        w_hi = {n: sb(f"w{n}_hi", [P, INNER], F32R) for n in "qkv"}
        w_lo = {n: sb(f"w{n}_lo", [P, INNER], F32R) for n in "qkv"}
        wo_sb = sb("wo_sb", [P, CHUNKS, P])
        router_sb = sb("router_sb", [P, E_ROUTED])
        act_scratch = sb("act_scratch", [P, 1])
        warm = sb("warm", [P, 512])
        carrier = sb("carrier", [P, 4])
        x_sb = sb("x_sb", [P, B, P])
        ctx_sb = sb("ctx_sb", [P, B * P])
        mask_sb = [sb(f"mask{i}", [P, P]) for i in range(2)]
        stats = sb("stats", [P, B, 6])
        moments = sb("moments", [P, B, 2])
        half_var, square, rstd = sb("half_var", [P, B]), sb("square", [P, B]), sb("rstd", [P, B])
        xn = sb("xn", [P, B, P])
        xT_hi, xT_lo = sb("xT_hi", [P, B * P], F32R), sb("xT_lo", [P, B * P], F32R)
        ck_hi, ck_lo = sb("ck_hi", [P, B * P], F32R), sb("ck_lo", [P, B * P], F32R)
        cv_hi, cv_lo = sb("cv_hi", [P, 2 * P], F32R), sb("cv_lo", [P, 2 * P], F32R)
        qT = sb("qT", [P, CHUNKS, 2 * P])
        kT = sb("kT", [P, CHUNKS, 2 * P])
        v_sb = [sb(f"v{i}", [P, INNER]) for i in range(2)]
        probs = sb("probs", [P, 4, 8, P])
        negmax = sb("negmax", [P, 4, 8])
        rowsum = sb("rowsum", [P, 4, 8])
        rinv = sb("rinv", [P, 4, 8])
        probsT = sb("probsT", [P, 2, 8, P])
        oT = sb("oT", [P, 2, 4, P])
        stats2 = sb("stats2", [P, 6])
        moments2 = sb("moments2", [P, 2])
        half_var2, square2, rstd2 = sb("half_var2", [P, 1]), sb("square2", [P, 1]), sb("rstd2", [P, 1])
        xn2T = sb("xn2T", [P, B * P])
        xn2T_hi, xn2T_lo = sb("xn2T_hi", [P, B * P], F32R), sb("xn2T_lo", [P, B * P], F32R)
        gu_raw = [sb(f"gu_raw{i}", [P, 2 * I_FFN]) for i in range(2)]
        gu_hi = [sb(f"gu_hi{i}", [P, 2 * I_FFN], F32R) for i in range(2)]
        gu_lo = [sb(f"gu_lo{i}", [P, 2 * I_FFN], F32R) for i in range(2)]
        down_sb = [sb(f"down{i}", [P, 2, P]) for i in range(2)]
        silu_sb = sb("silu_sb", [P, 2, 512])
        h_sb = sb("h_sb", [P, 2, 2, 512])
        z, ez, den, prob = (sb(n, [P, B, E_ROUTED]) for n in ("z", "ez", "den", "prob"))
        cand, hot1, hot2, prob2 = (sb(n, [P, B, E_ROUTED]) for n in ("cand", "hot1", "hot2", "prob2"))
        top1, top2, first, total = (sb(n, [P, B]) for n in ("top1", "top2", "first", "total"))
        w_all = sb("w_all", [P, EXPERTS, B])
        w_col = [sb(f"w_col{i}", [P, B]) for i in range(2)]

        s_bank = [bank("s_even"), bank("s_odd")]
        pt_bank = [bank("pt0"), bank("pt1")]
        proj_bank = {"q": bank("proj_q"), "k": bank("proj_k")}
        o_bank = bank("o_bank")
        misc = bank("misc")
        g_bank, u_bank = [s_bank[0], pt_bank[0]], [s_bank[1], pt_bank[1]]
        d_bank = [proj_bank["q"], proj_bank["k"]]

        in_x0, in_x, in_ctx0, in_ctx = sem("in_x0"), sem("in_x"), sem("in_ctx0"), sem("in_ctx")
        in_w = {n: [sem(f"in_w{n}0"), sem(f"in_w{n}1")] for n in "qkv"}
        in_wo, in_ident, in_rows, in_router = sem("in_wo"), sem("in_ident"), sem("in_rows"), sem("in_router")
        in_mask = [sem("in_mask0"), sem("in_mask1")]
        in_gu = [sem("in_gu0"), sem("in_gu1")]
        in_down = [sem("in_down0"), sem("in_down1")]
        out_sem = sem("out_sem")
        tanh_ready = sem("tanh_ready")
        whi_ready = {n: sem(f"w{n}hi_ready") for n in "qkv"}
        wlo_ready = {n: [sem(f"w{n}lo_ready{i}") for i in range(2)] for n in "qkv"}
        ckhi_ready, cklo_ready = sem("ckhi_ready"), sem("cklo_ready")
        ckhi_rest, cklo_rest = sem("ckhi_rest"), sem("cklo_rest")
        ln1_step, ln2_step = sem("ln1_step"), sem("ln2_step")
        xn_ready = sem("xn_ready")
        xn2_ready = sem("xn2_ready")
        xthi_ready = sem("xthi_ready")
        cvhi_ready, cvlo_ready = sem("cvhi_ready"), sem("cvlo_ready")
        misc_done, misc_free = sem("misc_done"), sem("misc_free")
        warm_ready = sem("warm_ready")
        q_done, q_free = sem("q_done"), sem("q_free")
        k_done, k_free = sem("k_done"), sem("k_free")
        s_done, ttr_done = sem("s_done"), sem("ttr_done")
        exp_done, rinv_ready, norm_done = sem("exp_done"), sem("rinv_ready"), sem("norm_done")
        t_done = sem("t_done")
        pt0_free, pt1_free = sem("pt0_free"), sem("pt1_free")
        o_done, ot_ready = sem("o_done"), sem("ot_ready")
        xn2t_ready, xn2hi_ready = sem("xn2t_ready"), sem("xn2hi_ready")
        carrier_ready = sem("carrier_ready")
        guhi_ready, gulo_ready = sem("guhi_ready"), sem("gulo_ready")
        gu_done, silu_done, h_done = sem("gu_done"), sem("silu_done"), sem("h_done")
        d_done, acc_done = sem("d_done"), sem("acc_done")
        wcol_ready = sem("wcol_ready")
        r_done, z_ready, ez_ready = sem("r_done"), sem("z_ready"), sem("ez_ready")
        route_step, shared_ready = sem("route_step"), sem("shared_ready")

        block = stack.enter_context(nc.Block())

        @block.sync
        def _(sp):
            def load_w(name, src, half):
                cols = slice(half * 512, (half + 1) * 512)
                sp.dma_start(w_raw[name][:, cols], src[:, cols]).then_inc(in_w[name][half], 16)

            load_w("k", wkT, 0)
            sp.dma_start(ctx_sb[:, 0:2 * P], ctxT[:, 0:2 * P]).then_inc(in_ctx0, 16)
            sp.dma_start(x_sb[:, 0:2, :], x[:, 0:2, :]).then_inc(in_x0, 16)
            load_w("k", wkT, 1)
            load_w("q", wqT, 0)
            load_w("q", wqT, 1)
            sp.dma_start(x_sb[:, 2:B, :], x[:, 2:B, :]).then_inc(in_x, 16)
            sp.dma_start(mask_sb[0][:], mask[0]).then_inc(in_mask[0], 16)
            load_w("v", wvT, 0)
            load_w("v", wvT, 1)
            sp.dma_start(ctx_sb[:, 2 * P:], ctxT[:, 2 * P:]).then_inc(in_ctx, 16)
            sp.dma_start(mask_sb[1][:], mask[1]).then_inc(in_mask[1], 16)
            sp.dma_start(wo_sb[:], woT).then_inc(in_wo, 16)
            sp.dma_start(router_sb[:], routerT).then_inc(in_router, 16)
            for e in range(2):
                sp.dma_start(gu_raw[e][:], gu[e]).then_inc(in_gu[e], 16)
                sp.dma_start(down_sb[e][:], down[e]).then_inc(in_down[e], 16)
            with sp.Fori(1, PAIRS) as p:
                for i in range(2):
                    sp.wait_ge(ttr_done, HEADS * (2 * p + i - 1))
                    sp.dma_start(mask_sb[i][:], mask[bass.ds(2 * p + i, 1)].rearrange("o q k -> (o q) k")).then_inc(in_mask[i], 16)

            def load_expert(e, i):
                sp.wait_ge(gulo_ready, e - 1)
                sp.dma_start(gu_raw[i][:], gu[bass.ds(e, 1)].rearrange("o h i -> (o h) i")).then_inc(in_gu[i], 16)
                sp.wait_ge(d_done, 2 * (e - 1))
                sp.dma_start(down_sb[i][:], down[bass.ds(e, 1)].rearrange("o i c h -> (o i) c h")).then_inc(in_down[i], 16)

            with sp.Fori(1, EXPERTS // 2) as q:
                load_expert(2 * q, 0)
                load_expert(2 * q + 1, 1)
            load_expert(EXPERTS - 1, 0)
            for half in range(2):
                sp.wait_ge(acc_done, 2 * (EXPERTS - 1) + half + 1)
                tiles = slice(half * B // 2, (half + 1) * B // 2)
                sp.dma_start(out[:, tiles, :], x_sb[:, tiles, :]).then_inc(out_sem, 16)
            sp.wait_ge(out_sem, 32)

        @block.tensor
        def _(pe):
            def three_pass(dst, a_hi, a_lo, b_hi, b_lo):
                pe.matmul(dst, a_hi, b_hi, start=True, stop=False)
                pe.matmul(dst, a_lo, b_hi, start=False, stop=False)
                return pe.matmul(dst, a_hi, b_lo, start=False, stop=True)

            def xn_transposes(batches, bank):
                for i, b in enumerate(batches):
                    mm = pe.transpose(bank[:, i * P:(i + 1) * P], xn[:, b, :], ident_sb[:])
                mm.then_inc(misc_done, 1)

            def project_unit(name, cols, u, at, done):
                hi, lo = (xT_hi, xT_lo) if name == "q" else (ck_hi, ck_lo)
                for c in (2 * u, 2 * u + 1):
                    w = slice(c * P, (c + 1) * P)
                    mm = three_pass(at[:, (c % 2) * 2 * P:(c % 2 + 1) * 2 * P], w_hi[name][:, w], w_lo[name][:, w],
                                    hi[:, cols], lo[:, cols])
                mm.then_inc(done, 1)

            def project(pair, u, name):
                free, done = (q_free, q_done) if name == "q" else (k_free, k_done)
                pe.wait_ge(free, PROJ_USES * pair + u)
                project_unit(name, bass.ds(pair * 2 * P, 2 * P), u, proj_bank[name], done)

            def project_v(pair, i):
                tok = slice(i * P, (i + 1) * P)
                pe.wait_ge(cvlo_ready, pair + 1)
                for half, (name, free, done) in enumerate((("q", q_free, q_done), ("k", k_free, k_done))):
                    pe.wait_ge(free, PROJ_USES * pair + 4 + i)
                    cols = slice(half * 512, (half + 1) * 512)
                    three_pass(proj_bank[name][:], cv_hi[:, tok], cv_lo[:, tok], w_hi["v"][:, cols],
                               w_lo["v"][:, cols]).then_inc(done, 1)

            def scores(g, pair, r, units=None):
                i, half = r // 2, r % 2
                q_units, k_units = units or (2 * half + 2, 2 * half + 2)
                pe.wait_ge(q_free, PROJ_USES * pair + q_units)
                pe.wait_ge(k_free, PROJ_USES * pair + k_units)
                if not (isinstance(g, int) and g == 0):
                    pe.wait_ge(ttr_done, 8 * g)
                for j in range(4):
                    for odd in range(2):
                        rows = slice(DK * odd, DK * (odd + 1))
                        mm = pe.matmul(s_bank[odd][:, j * P:(j + 1) * P], qT[rows, 4 * half + j, i * P:(i + 1) * P],
                                       kT[rows, 4 * half + j, i * P:(i + 1) * P], start=True, stop=True)
                mm.then_inc(s_done, 1)

            def transposes(g, r):
                for u, free in enumerate((pt0_free, pt1_free)):
                    pe.wait_ge(norm_done, 2 * g + u + 1)
                    if not (isinstance(g, int) and g == 0):
                        pe.wait_ge(free, g)
                    for j in range(4):
                        mm = pe.transpose(pt_bank[u][:, j * P:(j + 1) * P], probs[:, r, 4 * u + j, :], ident_sb[:])
                    mm.then_inc(t_done, 1)

            def values(g, pair, r):
                i, half = r // 2, r % 2
                pe.wait_ge(q_free, PROJ_USES * pair + 5 + i)
                pe.wait_ge(k_free, PROJ_USES * pair + 5 + i)
                pe.wait_ge(pt0_free, g + 1)
                pe.wait_ge(pt1_free, g + 1)
                if not (isinstance(g, int) and g == 0):
                    pe.wait_ge(ot_ready, g)
                for j in range(4):
                    for odd in range(2):
                        h = 8 * half + 2 * j + odd
                        mm = pe.matmul(o_bank[DK * odd:DK * (odd + 1), j * P:(j + 1) * P],
                                       v_sb[i][:, h * DK:(h + 1) * DK], probsT[:, half, 2 * j + odd, :],
                                       start=True, stop=True)
                mm.then_inc(o_done, 1)

            def out_project(b, use):
                pe.wait_ge(ot_ready, 2 * b + 2)
                pe.wait_ge(misc_free, use)
                for c in range(CHUNKS):
                    mm = pe.matmul(misc[:, 0:P], oT[:, c // 4, c % 4, :], wo_sb[:, c, :],
                                   start=(c == 0), stop=(c == CHUNKS - 1))
                mm.then_inc(misc_done, 1)

            def xn2_transposes(batches, use):
                pe.wait_ge(xn2_ready, batches[-1] + 1)
                pe.wait_ge(misc_free, use)
                xn_transposes(batches, misc)

            pe.wait_ge(warm_ready, 1)
            for _ in range(WARM_UP):
                pe.matmul(misc[:], warm[:, 0:P], warm[:], start=True, stop=True)
            first = slice(0, 2 * P)
            pe.wait_ge(cklo_ready, 1)
            pe.wait_ge(wlo_ready["k"][0], 1)
            project_unit("k", first, 0, proj_bank["k"], k_done)
            project_unit("k", first, 1, proj_bank["q"], q_done)
            pe.wait_ge(in_ident, 16)
            pe.wait_ge(xn_ready, 2)
            xn_transposes(range(2), misc)
            pe.wait_ge(wlo_ready["k"][1], 1)
            pe.wait_ge(k_free, 1)
            project_unit("k", first, 2, proj_bank["k"], k_done)
            pe.wait_ge(wlo_ready["q"][0], 1)
            pe.wait_ge(misc_free, 1)
            pe.wait_ge(q_free, 1)
            project_unit("q", first, 0, proj_bank["q"], q_done)
            pe.wait_ge(k_free, 2)
            project_unit("q", first, 1, proj_bank["k"], k_done)
            pe.wait_ge(q_free, 2)
            project_unit("k", first, 3, proj_bank["q"], q_done)
            pe.wait_ge(wlo_ready["q"][1], 1)
            pe.wait_ge(k_free, 3)
            project_unit("q", first, 2, proj_bank["k"], k_done)
            scores(0, 0, 0, units=(2, 3))
            pe.wait_ge(q_free, 3)
            project_unit("q", first, 3, proj_bank["q"], q_done)
            pe.wait_ge(wlo_ready["v"][0], 1)
            pe.wait_ge(wlo_ready["v"][1], 1)
            project_v(0, 0)
            scores(1, 0, 1, units=(4, 4))
            pe.wait_ge(xn_ready, B)
            xn_transposes(range(2, 6), misc)
            xn_transposes(range(6, B), o_bank)
            transposes(0, 0)
            scores(2, 0, 2)
            project_v(0, 1)
            pe.wait_ge(misc_free, XT_USES + 1)
            values(0, 0, 0)
            pe.wait_ge(in_wo, 16)
            pe.wait_ge(cklo_rest, 1)

            with pe.Fori(0, PAIRS - 1) as p:
                g = 4 * p
                use = XT_USES + 1 + 2 * p
                transposes(g + 1, 1)
                scores(g + 3, p, 3)
                project(p + 1, 0, "q")
                project(p + 1, 0, "k")
                values(g + 1, p, 1)
                project(p + 1, 1, "q")
                project(p + 1, 1, "k")
                transposes(g + 2, 2)
                out_project(2 * p, use)
                scores(g + 4, p + 1, 0)
                project(p + 1, 2, "q")
                project(p + 1, 2, "k")
                values(g + 2, p, 2)
                project(p + 1, 3, "q")
                project(p + 1, 3, "k")
                transposes(g + 3, 3)
                scores(g + 5, p + 1, 1)
                project_v(p + 1, 0)
                values(g + 3, p, 3)
                transposes(g + 4, 0)
                out_project(2 * p + 1, use + 1)
                scores(g + 6, p + 1, 2)
                project_v(p + 1, 1)
                values(g + 4, p + 1, 0)

            def gate_up(n, i, half, c):
                tok = slice(half * 512, (half + 1) * 512)
                for dst, at in ((g_bank[c], c * P), (u_bank[c], I_FFN + c * P)):
                    mm = three_pass(dst[:], gu_hi[i][:, at:at + P], gu_lo[i][:, at:at + P], xn2T_hi[:, tok], xn2T_lo[:, tok])
                mm.then_inc(gu_done, 1)

            def down_step(j, i, half):
                pe.wait_ge(h_done, 2 * j + 2)
                for t in range(4):
                    for c in range(2):
                        mm = pe.matmul(d_bank[half][:, t * P:(t + 1) * P], h_sb[:, half, c, t * P:(t + 1) * P],
                                       down_sb[i][:, c, :], start=(c == 0), stop=(c == 1))
                mm.then_inc(d_done, 1)

            last = PAIRS - 1
            use = XT_USES + B - 1
            transposes(13, 1)
            scores(15, last, 3)
            values(13, last, 1)
            xn2_transposes(range(4), use)
            transposes(14, 2)
            out_project(B - 2, use + 1)
            values(14, last, 2)
            transposes(15, 3)
            xn2_transposes(range(4, B - 1), use + 2)
            values(15, last, 3)
            pe.wait_ge(gulo_ready, 1)
            pe.wait_ge(ttr_done, 8 * GROUPS)
            gate_up(0, 0, 0, 0)
            out_project(B - 1, use + 3)
            gate_up(1, 0, 0, 1)
            pe.wait_ge(in_down[0], 16)
            down_step(0, 0, 0)
            xn2_transposes(range(B - 1, B), use + 4)
            pe.wait_ge(h_done, 1)
            pe.wait_ge(misc_free, use + 5)
            pe.wait_ge(in_router, 16)
            for t in range(B):
                mm = pe.matmul(misc[:, t * E_ROUTED:(t + 1) * E_ROUTED], xn2T[:, t * P:(t + 1) * P], router_sb[:],
                               start=True, stop=True)
            mm.then_inc(r_done, 1)
            gate_up(2, 0, 1, 0)
            pe.wait_ge(h_done, 2)
            gate_up(3, 0, 1, 1)

            with pe.Fori(0, E_ROUTED // 2) as q:
                for s in range(4):
                    j = 4 * q + 2 + s
                    i = (s // 2 + 1) % 2
                    if s % 2 == 0:
                        pe.wait_ge(gulo_ready, 2 * q + 2 + s // 2)
                    for c in range(2):
                        pe.wait_ge(h_done, 2 * j + c - 1)
                        gate_up(2 * j + c, i, s % 2, c)
                    if s % 2 == 1:
                        pe.wait_ge(in_down[i], 16 * (q + 1 if i else q + 2))
                    pe.wait_ge(acc_done, j - 1)
                    down_step(j - 1, i if s % 2 else 1 - i, 1 - s % 2)
            pe.wait_ge(acc_done, 2 * EXPERTS - 2)
            down_step(2 * EXPERTS - 1, 0, 1)

        @block.scalar
        def _(act):
            act.wait_ge(warm_ready, 1)
            act.activation(act_scratch[:], warm[:, 0:1], ACT.Exp)

            def split_hi(name, half):
                act.wait_ge(in_w[name][half], 16)
                cols = slice(half * 512, (half + 1) * 512)
                act.copy(w_hi[name][:, cols], w_raw[name][:, cols]).then_inc(whi_ready[name], 1)

            def xT_hi_part(n, batches, bank):
                act.wait_ge(misc_done, n)
                act.copy(xT_hi[:, batches[0] * P:(batches[-1] + 1) * P], bank[:, 0:len(batches) * P]).then_inc(xthi_ready, 1)

            def copy_q(pair, u):
                act.wait_ge(q_done, PROJ_USES * pair + u + 1)
                act.copy(qT[:, 2 * u:2 * u + 2, :].rearrange("p c t -> p (c t)"), proj_bank["q"][:]).then_inc(q_free, 1)

            def copy_v(pair, i):
                act.wait_ge(q_done, PROJ_USES * pair + 5 + i)
                act.copy(v_sb[i][:, 0:512], proj_bank["q"][:]).then_inc(q_free, 1)

            def exps(g, r, u):
                for l in range(4 * u, 4 * u + 4):
                    act.wait_ge(ttr_done, 8 * g + l + 1)
                    e = act.activation(probs[:, r, l, :], probs[:, r, l, :], ACT.Exp, bias=negmax[:, r, l:l + 1],
                                       scale=-1.0, accum_out=rowsum[:, r, l:l + 1])
                e.then_inc(exp_done, 1)

            def copy_pt(g, r):
                act.wait_ge(t_done, 2 * g + 1)
                act.copy(probsT[:, r % 2, 0:4, :].rearrange("p h q -> p (h q)"), pt_bank[0][:]).then_inc(pt0_free, 1)

            def copy_xn2T(batches, use):
                act.wait_ge(misc_done, use + 1)
                cols, n = slice(batches[0] * P, (batches[-1] + 1) * P), len(batches) * P
                act.copy(xn2T_hi[:, cols], misc[:, 0:n]).then_inc(xn2hi_ready, 1)
                act.copy(xn2T[:, cols], misc[:, 0:n]).then_inc(xn2t_ready, 1)

            split_hi("k", 0)
            act.wait_ge(in_ctx0, 16)
            act.copy(ck_hi[:, 0:2 * P], ctx_sb[:, 0:2 * P]).then_inc(ckhi_ready, 1)
            split_hi("k", 1)
            split_hi("q", 0)
            split_hi("q", 1)

            def copy_first(dst, u, n):
                act.wait_ge(q_done, n)
                act.copy(dst[:, 2 * u:2 * u + 2, :].rearrange("p c t -> p (c t)"), proj_bank["q"][:]).then_inc(q_free, 1)

            copy_first(kT, 1, 1)
            xT_hi_part(1, range(2), misc)
            split_hi("v", 0)
            split_hi("v", 1)
            copy_first(qT, 0, 2)
            copy_first(kT, 3, 3)
            act.wait_ge(in_rows, 16)
            act.activation(tanh_g[:], gates, ACT.Tanh).then_inc(tanh_ready, 1)
            copy_first(qT, 3, 4)
            exps(0, 0, 0)
            copy_v(0, 0)
            exps(0, 0, 1)
            xT_hi_part(2, range(2, 6), misc)
            xT_hi_part(3, range(6, B), o_bank)
            exps(1, 1, 0)
            exps(1, 1, 1)
            copy_pt(0, 0)
            copy_v(0, 1)
            exps(2, 2, 0)
            exps(2, 2, 1)

            with act.Fori(0, PAIRS - 1) as p:
                g = 4 * p
                use = XT_USES + 1 + 2 * p
                copy_pt(g + 1, 1)
                copy_q(p + 1, 0)
                exps(g + 3, 3, 0)
                copy_q(p + 1, 1)
                exps(g + 3, 3, 1)
                copy_pt(g + 2, 2)
                copy_q(p + 1, 2)
                exps(g + 4, 0, 0)
                copy_q(p + 1, 3)
                exps(g + 4, 0, 1)
                copy_pt(g + 3, 3)
                exps(g + 5, 1, 0)
                copy_v(p + 1, 0)
                exps(g + 5, 1, 1)
                copy_pt(g + 4, 0)
                exps(g + 6, 2, 0)
                copy_v(p + 1, 1)
                exps(g + 6, 2, 1)

            def silu(n, c):
                act.wait_ge(gu_done, n + 1)
                act.activation(silu_sb[:, c, :], g_bank[c][:], ACT.Silu).then_inc(silu_done, 1)

            use = XT_USES + B - 1
            copy_pt(13, 1)
            exps(15, 3, 0)
            exps(15, 3, 1)
            copy_xn2T(range(4), use)
            copy_pt(14, 2)
            copy_pt(15, 3)
            copy_xn2T(range(4, B - 1), use + 2)
            silu(0, 0)
            silu(1, 1)
            copy_xn2T(range(B - 1, B), use + 4)
            silu(2, 0)
            silu(3, 1)
            act.wait_ge(z_ready, 1)
            act.activation(ez[:], z[:], ACT.Exp, scale=-1.0).then_inc(ez_ready, 1)
            with act.Fori(0, E_ROUTED // 2) as q:
                for s in range(4):
                    for c in range(2):
                        silu(8 * q + 4 + 2 * s + c, c)

        @block.vector
        def _(dve):
            def carry_wait(column):
                dve.memset(carrier[:, column:column + 1], 0.0)

            def norm1_steps(tiles, n):
                a, b = tiles[0], tiles[-1] + 1
                var, sq, y = half_var[:, a:b], square[:, a:b], rstd[:, a:b]
                for t in tiles:
                    dve.bn_stats(stats[:, t, :], x_sb[:, t, :]).then_inc(ln1_step, 1)
                    yield
                n += b - a
                dve.wait_ge(ln1_step, n)
                for t in tiles:
                    dve.bn_aggr(moments[:, t, :], stats[:, t, :]).then_inc(ln1_step, 1)
                yield
                n += b - a
                dve.wait_ge(ln1_step, n)
                dve.tensor_scalar(var, moments[:, a:b, 1], EPS, -0.5, ALU.add, ALU.mult).then_inc(ln1_step, 1)
                yield
                dve.wait_ge(ln1_step, n + 1)
                dve.tensor_scalar(y.bitcast(I32), var.bitcast(I32), -0.5, SEED, ALU.mult, ALU.add).then_inc(ln1_step, 1)
                yield
                n += 2
                for _ in range(NEWTON):
                    dve.wait_ge(ln1_step, n)
                    dve.tensor_tensor(sq, y, y, ALU.mult).then_inc(ln1_step, 1)
                    yield
                    dve.wait_ge(ln1_step, n + 1)
                    dve.tensor_tensor(sq, sq, var, ALU.mult).then_inc(ln1_step, 1)
                    yield
                    dve.wait_ge(ln1_step, n + 2)
                    dve.scalar_tensor_tensor(y, sq, 1.5, y, ALU.add, ALU.mult).then_inc(ln1_step, 1)
                    yield
                    n += 3
                dve.wait_ge(ln1_step, n)
                for t in tiles:
                    dve.tensor_scalar(xn[:, t, :], x_sb[:, t, :], moments[:, t, 0:1], rstd[:, t:t + 1],
                                      ALU.subtract, ALU.mult).then_inc(xn_ready, 1)
                    yield

            def split_lo(name, half):
                dve.wait_ge(whi_ready[name], half + 1)
                cols = slice(half * 512, (half + 1) * 512)
                dve.tensor_tensor(w_lo[name][:, cols], w_raw[name][:, cols], w_hi[name][:, cols].bitcast(F32),
                                  ALU.subtract).then_inc(wlo_ready[name][half], 1)

            def xT_lo_part(n, batches, bank):
                dve.wait_ge(xthi_ready, n)
                cols = slice(batches[0] * P, (batches[-1] + 1) * P)
                dve.tensor_tensor(xT_lo[:, cols], bank[:, 0:len(batches) * P], xT_hi[:, cols].bitcast(F32),
                                  ALU.subtract).then_inc(misc_free, 1)

            def copy_k(pair, u):
                dve.wait_ge(k_done, PROJ_USES * pair + u + 1)
                dve.tensor_copy(kT[:, 2 * u:2 * u + 2, :].rearrange("p c t -> p (c t)"), proj_bank["k"][:]).then_inc(k_free, 1)

            def copy_v(pair, i):
                dve.wait_ge(k_done, PROJ_USES * pair + 5 + i)
                dve.tensor_copy(v_sb[i][:, 512:], proj_bank["k"][:]).then_inc(k_free, 1)

            def mask_max(g, b2, r, between=iter(())):
                dve.wait_ge(s_done, g + 1)
                dve.wait_ge(in_mask[r // 2], 16 * (b2 + 1))
                carry_wait(0)
                for l in range(8):
                    dve.tensor_tensor_reduce(probs[:, r, l, :], s_bank[l % 2][:, (l // 2) * P:(l // 2 + 1) * P],
                                             mask_sb[r // 2][:], -1.0, HUGE, ALU.add, ALU.min,
                                             negmax[:, r, l:l + 1]).then_inc(ttr_done, 1)
                    next(between, None)

            def recips(g, r, quads=(0, 1)):
                for u in quads:
                    dve.wait_ge(exp_done, 2 * g + u + 1)
                    dve.reciprocal(rinv[:, r, 4 * u:4 * u + 4], rowsum[:, r, 4 * u:4 * u + 4]).then_inc(rinv_ready, 1)

            def copy_pt(g, r):
                dve.wait_ge(t_done, 2 * g + 2)
                dve.tensor_copy(probsT[:, r % 2, 4:8, :].rearrange("p h q -> p (h q)"), pt_bank[1][:]).then_inc(pt1_free, 1)

            def copy_o(g, r):
                dve.wait_ge(o_done, g + 1)
                dve.tensor_copy(oT[:, r % 2, :, :].rearrange("p c q -> p (c q)"), o_bank[:]).then_inc(ot_ready, 1)

            def x_of(b):
                return x_sb[:, bass.ds(b, 1), :].rearrange("p o d -> p (o d)")

            def add_attention(b, use):
                dve.wait_ge(misc_done, use + 1)
                dve.scalar_tensor_tensor(x_of(b), misc[:, 0:P], tanh_g[:, 0:1], x_of(b), ALU.mult, ALU.add).then_inc(misc_free, 1)

            def norm2_steps(b, use):
                n = LN2_STEPS * b
                dve.wait_ge(misc_free, use + 1)
                carry_wait(1)
                dve.bn_stats(stats2[:], x_of(b)).then_inc(ln2_step, 1)
                yield
                dve.wait_ge(ln2_step, n + 1)
                carry_wait(1)
                dve.bn_aggr(moments2[:], stats2[:]).then_inc(ln2_step, 1)
                yield
                dve.wait_ge(ln2_step, n + 2)
                dve.tensor_scalar(half_var2[:], moments2[:, 1:2], EPS, -0.5, ALU.add, ALU.mult).then_inc(ln2_step, 1)
                yield
                dve.wait_ge(ln2_step, n + 3)
                dve.tensor_scalar(rstd2[:].bitcast(I32), half_var2[:].bitcast(I32), -0.5, SEED, ALU.mult,
                                  ALU.add).then_inc(ln2_step, 1)
                yield
                for k in range(NEWTON):
                    dve.wait_ge(ln2_step, n + 4 + 2 * k)
                    dve.tensor_scalar(square2[:], rstd2[:], rstd2[:], half_var2[:], ALU.mult, ALU.mult).then_inc(ln2_step, 1)
                    yield
                    dve.wait_ge(ln2_step, n + 5 + 2 * k)
                    dve.scalar_tensor_tensor(rstd2[:], square2[:], 1.5, rstd2[:], ALU.add, ALU.mult).then_inc(ln2_step, 1)
                    yield
                dve.wait_ge(ln2_step, n + LN2_STEPS)
                xn_b = xn[:, bass.ds(b, 1), :].rearrange("p o d -> p (o d)")
                dve.tensor_scalar(xn_b, x_of(b), moments2[:, 0:1], rstd2[:], ALU.subtract, ALU.mult).then_inc(xn2_ready, 1)
                yield

            def run(steps, count):
                for _ in range(count):
                    next(steps, None)

            def finish(steps):
                for _ in steps:
                    pass

            def xn2T_lo_part(n, batches):
                dve.wait_ge(xn2hi_ready, n)
                dve.wait_ge(xn2t_ready, n)
                cols = slice(batches[0] * P, (batches[-1] + 1) * P)
                dve.tensor_tensor(xn2T_lo[:, cols], misc[:, 0:len(batches) * P], xn2T_hi[:, cols].bitcast(F32),
                                  ALU.subtract).then_inc(misc_free, 1)

            def copy_first(dst, u, n):
                dve.wait_ge(k_done, n)
                dve.tensor_copy(dst[:, 2 * u:2 * u + 2, :].rearrange("p c t -> p (c t)"), proj_bank["k"][:]).then_inc(k_free, 1)

            dve.memset(warm[:], 0.0).then_inc(warm_ready, 1)
            split_lo("k", 0)
            dve.wait_ge(ckhi_ready, 1)
            dve.tensor_tensor(ck_lo[:, 0:2 * P], ctx_sb[:, 0:2 * P], ck_hi[:, 0:2 * P].bitcast(F32),
                              ALU.subtract).then_inc(cklo_ready, 1)
            dve.wait_ge(in_x0, 16)
            finish(norm1_steps(range(2), 0))
            copy_first(kT, 0, 1)
            split_lo("q", 0)
            xT_lo_part(1, range(2), misc)
            dve.wait_ge(in_x, 16)
            steps = norm1_steps(range(2, B), 4 + 2 + 3 * NEWTON)
            run(steps, 2)
            copy_first(kT, 2, 2)
            run(steps, 5)
            copy_first(qT, 1, 3)
            run(steps, 4)
            copy_first(qT, 2, 4)
            run(steps, 4)
            mask_max(0, 0, 0, islice(steps, 3))
            finish(steps)
            copy_v(0, 0)
            recips(0, 0)
            mask_max(1, 0, 1)
            xT_lo_part(2, range(2, 6), misc)
            xT_lo_part(3, range(6, B), o_bank)
            recips(1, 1, (0,))
            recips(1, 1, (1,))
            copy_pt(0, 0)
            mask_max(2, 0, 2)
            copy_v(0, 1)
            copy_o(0, 0)
            recips(2, 2)
            dve.wait_ge(tanh_ready, 1)

            with dve.Fori(0, PAIRS - 1) as p:
                g = 4 * p
                use = XT_USES + 1 + 2 * p
                copy_pt(g + 1, 1)
                mask_max(g + 3, p, 3)
                copy_k(p + 1, 0)
                copy_o(g + 1, 1)
                recips(g + 3, 3)
                copy_k(p + 1, 1)
                copy_pt(g + 2, 2)
                add_attention(2 * p, use)
                mask_max(g + 4, p + 1, 0)
                copy_k(p + 1, 2)
                copy_o(g + 2, 2)
                copy_k(p + 1, 3)
                recips(g + 4, 0)
                copy_pt(g + 3, 3)
                steps = norm2_steps(2 * p, use)
                mask_max(g + 5, p + 1, 1, steps)
                copy_o(g + 3, 3)
                run(steps, 1)
                copy_v(p + 1, 0)
                run(steps, 1)
                recips(g + 5, 1)
                finish(steps)
                copy_pt(g + 4, 0)
                add_attention(2 * p + 1, use + 1)
                steps = norm2_steps(2 * p + 1, use + 1)
                mask_max(g + 6, p + 1, 2, steps)
                copy_o(g + 4, 0)
                run(steps, 1)
                copy_v(p + 1, 1)
                run(steps, 1)
                recips(g + 6, 2)
                finish(steps)

            def hidden(n, half, c):
                dve.wait_ge(silu_done, n + 1)
                dve.tensor_tensor(h_sb[:, half, c, :], silu_sb[:, c, :], u_bank[c][:], ALU.mult).then_inc(h_done, 1)

            def column(e, i):
                dve.tensor_copy(w_col[i][:], w_all[:, bass.ds(e, 1), :].rearrange("p o t -> p (o t)")).then_inc(wcol_ready, 1)

            def add_expert(j, e, i, half):
                dve.wait_ge(d_done, j + 1)
                dve.wait_ge(wcol_ready, e + 1)
                if not (isinstance(j, int) and j < 2):
                    dve.wait_ge(acc_done, j - 1)
                for t in range(4):
                    tile = 4 * half + t
                    a = dve.scalar_tensor_tensor(x_sb[:, tile, :], d_bank[half][:, t * P:(t + 1) * P],
                                                 w_col[i][:, tile:tile + 1], x_sb[:, tile, :], ALU.mult, ALU.add)
                a.then_inc(acc_done, 1)

            use = XT_USES + B - 1
            copy_pt(13, 1)
            mask_max(15, PAIRS - 1, 3)
            copy_o(13, 1)
            recips(15, 3)
            xn2T_lo_part(1, range(4))
            copy_pt(14, 2)
            add_attention(B - 2, use + 1)
            steps = norm2_steps(B - 2, use + 1)
            run(steps, 2)
            copy_o(14, 2)
            run(steps, 4)
            finish(steps)
            copy_pt(15, 3)
            copy_o(15, 3)
            xn2T_lo_part(2, range(4, B - 1))
            dve.tensor_copy(w_all[:, 0, :], tanh_g[:, 1:2].to_broadcast([P, B])).then_inc(shared_ready, 1)
            dve.wait_ge(shared_ready, 1)
            column(0, 0)
            hidden(0, 0, 0)
            add_attention(B - 1, use + 3)
            steps = norm2_steps(B - 1, use + 3)
            run(steps, 8)
            hidden(1, 0, 1)
            finish(steps)
            xn2T_lo_part(3, range(B - 1, B))
            add_expert(0, 0, 0, 0)
            dve.wait_ge(in_rows, 16)
            dve.wait_ge(r_done, 1)
            dve.tensor_tensor(z[:], misc[:, 0:B * E_ROUTED].rearrange("p (t e) -> p t e", t=B),
                              bias_sb.unsqueeze(1).to_broadcast([P, B, E_ROUTED]), ALU.add).then_inc(z_ready, 1)
            hidden(2, 1, 0)
            hidden(3, 1, 1)

            def tiles(a):
                return a[:].unsqueeze(2).to_broadcast([P, B, E_ROUTED])

            def routing_steps():
                done = [0]

                def chained(instruction):
                    done[0] += 1
                    instruction.then_inc(route_step, 1)
                    return done[0]

                def first_of(values, top, hot):
                    yield chained(dve.tensor_reduce(top[:], values[:], AX, ALU.max))
                    yield chained(dve.tensor_tensor(cand[:], values[:], tiles(top), ALU.is_equal))
                    yield chained(dve.tensor_tensor(cand[:], cand[:], iota_sb.unsqueeze(1).to_broadcast([P, B, E_ROUTED]), ALU.mult))
                    yield chained(dve.tensor_reduce(first[:], cand[:], AX, ALU.min))
                    yield chained(dve.tensor_tensor(hot[:], cand[:], tiles(first), ALU.is_equal))

                yield chained(dve.tensor_scalar(den[:], ez[:], 1.0, None, ALU.add))
                yield chained(dve.reciprocal(prob[:], den[:]))
                yield from first_of(prob, top1, hot1)
                yield chained(dve.scalar_tensor_tensor(prob2[:], hot1[:], -2.0, prob[:], ALU.mult, ALU.add))
                yield from first_of(prob2, top2, hot2)
                yield chained(dve.tensor_tensor(total[:], top1[:], top2[:], ALU.add))
                yield chained(dve.reciprocal(total[:], total[:]))
                yield chained(dve.tensor_scalar(total[:], total[:], tanh_g[:, 1:2], None, ALU.mult))
                yield chained(dve.tensor_tensor(hot1[:], hot1[:], tiles(top1), ALU.mult))
                yield chained(dve.tensor_tensor(hot2[:], hot2[:], tiles(top2), ALU.mult))
                yield chained(dve.tensor_tensor(hot1[:], hot1[:], hot2[:], ALU.add))
                yield chained(dve.tensor_tensor(w_all[:, 1:, :].rearrange("p e t -> p t e"), hot1[:], tiles(total), ALU.mult))

            ROUTING_STEPS = 20

            def run_routing(steps, count):
                for _ in range(count):
                    n = next(steps, None)
                    if n is not None:
                        dve.wait_ge(route_step, n)

            def two_experts(q, routing=iter(())):
                for s in range(4):
                    j = 4 * q + 2 + s
                    for c in range(2):
                        hidden(2 * j + c, s % 2, c)
                        run_routing(routing, ROUTING_STEPS // 3)
                    i = (s // 2 + 1) % 2
                    e = 2 * q + 1 + s // 2
                    if s % 2:
                        run_routing(routing, ROUTING_STEPS)
                        dve.wait_ge(route_step, ROUTING_STEPS)
                        column(e, i)
                        add_expert(j - 1, e, i, 0)
                    else:
                        add_expert(j - 1, e - 1, 1 - i, 1)

            routing = routing_steps()
            dve.wait_ge(ez_ready, 1)
            run_routing(routing, ROUTING_STEPS // 3)
            two_experts(0, routing)
            with dve.Fori(1, E_ROUTED // 2) as q:
                two_experts(q)
            add_expert(2 * EXPERTS - 1, E_ROUTED, 0, 1)

        @block.gpsimd
        def _(pool):
            pool.memset(carrier[:, 2:3], 0.0).then_inc(carrier_ready, 1)
            pool.wait_ge(carrier_ready, 1)

            def carry_wait():
                pool.tensor_tensor(carrier[:, 3:4], carrier[:, 2:3], carrier[:, 2:3], ALU.add)

            def split_ctx(pair):
                cols = bass.ds(pair * 2 * P, 2 * P)
                pool.tensor_copy(cv_hi[:], ctx_sb[:, cols]).then_inc(cvhi_ready, 1)
                pool.wait_ge(cvhi_ready, pair + 1)
                carry_wait()
                pool.tensor_tensor(cv_lo[:], ctx_sb[:, cols], cv_hi[:].bitcast(F32), ALU.subtract).then_inc(cvlo_ready, 1)

            def split_lo(name, half):
                pool.wait_ge(whi_ready[name], half + 1)
                cols = slice(half * 512, (half + 1) * 512)
                pool.tensor_tensor(w_lo[name][:, cols], w_raw[name][:, cols], w_hi[name][:, cols].bitcast(F32),
                                   ALU.subtract).then_inc(wlo_ready[name][half], 1)

            def normalise(g, r):
                for u in range(2):
                    quad = probs[:, r, 4 * u:4 * u + 4, :]
                    pool.wait_ge(rinv_ready, 2 * g + u + 1)
                    pool.tensor_tensor(quad, quad, rinv[:, r, 4 * u:4 * u + 4].unsqueeze(2).to_broadcast([P, 4, P]),
                                       ALU.mult).then_inc(norm_done, 1)

            def split_expert(e, i, n):
                pool.wait_ge(in_gu[i], 16 * n)
                carry_wait()
                pool.tensor_copy(gu_hi[i][:], gu_raw[i][:]).then_inc(guhi_ready, 1)
                pool.wait_ge(guhi_ready, e + 1)
                pool.tensor_tensor(gu_lo[i][:], gu_raw[i][:], gu_hi[i][:].bitcast(F32), ALU.subtract).then_inc(gulo_ready, 1)

            pool.dma_start(ident_sb[:], ident).then_inc(in_ident, 16)
            pool.dma_start(rows_sb[:], rows.partition_broadcast(P)).then_inc(in_rows, 16)
            split_lo("k", 1)
            split_lo("q", 1)
            pool.wait_ge(in_ctx0, 16)
            split_ctx(0)
            split_lo("v", 0)
            split_lo("v", 1)
            pool.wait_ge(in_ctx, 16)
            pool.tensor_copy(ck_hi[:, 2 * P:], ctx_sb[:, 2 * P:]).then_inc(ckhi_rest, 1)
            pool.wait_ge(ckhi_rest, 1)
            pool.tensor_tensor(ck_lo[:, 2 * P:], ctx_sb[:, 2 * P:], ck_hi[:, 2 * P:].bitcast(F32),
                               ALU.subtract).then_inc(cklo_rest, 1)
            for g in range(3):
                normalise(g, g)
            with pool.Fori(0, PAIRS - 1) as p:
                normalise(4 * p + 3, 3)
                pool.wait_ge(k_done, PROJ_USES * (p + 1))
                carry_wait()
                split_ctx(p + 1)
                for r in range(3):
                    normalise(4 * p + 4 + r, r)
            split_expert(0, 0, 1)
            normalise(GROUPS - 1, 3)
            split_expert(1, 1, 1)

            def next_expert(e, i, n):
                pool.wait_ge(gu_done, 4 * (e - 1))
                split_expert(e, i, n)

            with pool.Fori(1, EXPERTS // 2) as q:
                next_expert(2 * q, 0, q + 1)
                next_expert(2 * q + 1, 1, q + 1)
            next_expert(EXPERTS - 1, 0, EXPERTS // 2 + 1)


def kernel(x, ctx_1024, fside_Bx1xSxS2_0, g_xattn, g_ffn, L0_xattn_Wq, L0_xattn_Wk, L0_xattn_Wv, L0_xattn_Wo,
           L0_ffn_shared_gate, L0_ffn_shared_up, L0_ffn_shared_down, L0_ffn_gate_w, L0_ffn_up_w, L0_ffn_down_w,
           L0_ffn_router_w, L0_ffn_routing_bias):
    import numpy as np
    import concourse.bacc as bacc
    from concourse.bass_utils import run_bass_kernel_spmd

    a = np.asarray
    wo = a(L0_xattn_Wo).T.reshape(CHUNKS, P, P).transpose(1, 0, 2)
    gate = np.concatenate([a(L0_ffn_shared_gate).T[None], a(L0_ffn_gate_w)])
    up = np.concatenate([a(L0_ffn_shared_up).T[None], a(L0_ffn_up_w)])
    down = np.concatenate([a(L0_ffn_shared_down).T[None], a(L0_ffn_down_w)])
    arrays = {
        "x": a(x).transpose(1, 0, 2),
        "ctxT": a(ctx_1024).transpose(2, 0, 1).reshape(P, B * P),
        "mask": a(fside_Bx1xSxS2_0).reshape(B, P, P),
        "wqT": a(L0_xattn_Wq).T,
        "wkT": a(L0_xattn_Wk).T,
        "wvT": a(L0_xattn_Wv).T,
        "woT": wo,
        "gu": np.concatenate([gate, up], axis=2),
        "down": down.reshape(EXPERTS, 2, P, P).transpose(0, 2, 1, 3),
        "routerT": a(L0_ffn_router_w).T,
        "rows": np.concatenate([a(g_xattn), a(g_ffn), a(L0_ffn_routing_bias), np.arange(-E_ROUTED, 0, dtype=np.float32)]),
        "ident": np.eye(P, dtype=np.float32),
    }
    arrays = {n: np.ascontiguousarray(v) for n, v in arrays.items()}
    nc = bacc.Bacc("TRN2", target_bir_lowering=False, num_devices=1)
    args = {n: nc.dram_tensor(n, v.shape, mybir.dt.from_np(v.dtype), kind="ExternalInput").ap() for n, v in arrays.items()}
    args["out"] = nc.dram_tensor("out", (P, B, P), F32, kind="ExternalOutput").ap()
    build(nc, **args)
    result = run_bass_kernel_spmd(nc, [arrays], core_ids=[0])
    return result.results[0]["out"].transpose(1, 0, 2)
```

```python
from contextlib import ExitStack
from itertools import islice

import concourse.bass as bass
from concourse import mybir

ALU = mybir.AluOpType
ACT = mybir.ActivationFunctionType
F32 = mybir.dt.float32
F32R = mybir.dt.float32r
I32 = mybir.dt.int32
AX = mybir.AxisListType.X

P = 128
B = 8
HEADS = 16
DK = 64
INNER = HEADS * DK
CHUNKS = INNER // P
PAIRS = B // 2
GROUPS = 2 * B
E_ROUTED = 8
EXPERTS = E_ROUTED + 1
STEPS = 2 * EXPERTS
I_FFN = 256
EPS = 1e-5
HUGE = 3.0e38

PROJ_USES = 6
XT_USES = 2
LN2_STEPS = 10
SEED = float(0x5EF759DF - (1 << 30))
NEWTON = 3
WARM_UP = 10


def build(nc, x, ctxT, mask, wqT, wkT, wvT, woT, gu, down, routerT, rows, ident, out):
    with ExitStack() as stack:
        def sb(name, shape, dt=F32):
            return stack.enter_context(nc.sbuf_tensor(name, shape, dt))

        def bank(name):
            return stack.enter_context(nc.psum_tensor(name, [P, 512], F32))

        def sem(name):
            return stack.enter_context(nc.semaphore(name))

        ident_sb = sb("ident_sb", [P, P])
        rows_sb = sb("rows_sb", [P, 2 * E_ROUTED + 2])
        gates, bias_sb, iota_sb = rows_sb[:, 0:2], rows_sb[:, 2:2 + E_ROUTED], rows_sb[:, 2 + E_ROUTED:]
        tanh_g = sb("tanh_g", [P, 2])
        w_raw = {n: sb(f"w{n}_raw", [P, INNER]) for n in "qkv"}
        w_hi = {n: sb(f"w{n}_hi", [P, INNER], F32R) for n in "qkv"}
        w_lo = {n: sb(f"w{n}_lo", [P, INNER], F32R) for n in "qkv"}
        wo_sb = sb("wo_sb", [P, CHUNKS, P])
        router_sb = sb("router_sb", [P, E_ROUTED])
        act_scratch = sb("act_scratch", [P, 1])
        warm = sb("warm", [P, P])
        carrier = sb("carrier", [P, 4])
        x_sb = sb("x_sb", [P, B, P])
        ctx_sb = sb("ctx_sb", [P, B * P])
        mask_sb = [sb(f"mask{i}", [P, P]) for i in range(2)]
        stats = sb("stats", [P, B, 6])
        moments = sb("moments", [P, B, 2])
        half_var, square, rstd = sb("half_var", [P, B]), sb("square", [P, B]), sb("rstd", [P, B])
        xn = sb("xn", [P, B, P])
        xT_hi, xT_lo = sb("xT_hi", [P, B * P], F32R), sb("xT_lo", [P, B * P], F32R)
        ck_hi, ck_lo = sb("ck_hi", [P, B * P], F32R), sb("ck_lo", [P, B * P], F32R)
        cv_hi, cv_lo = sb("cv_hi", [P, 2 * P], F32R), sb("cv_lo", [P, 2 * P], F32R)
        qT = sb("qT", [P, CHUNKS, 2 * P])
        kT = sb("kT", [P, CHUNKS, 2 * P])
        v_sb = [sb(f"v{i}", [P, INNER]) for i in range(2)]
        probs = sb("probs", [P, 4, 8, P])
        negmax = sb("negmax", [P, 4, 8])
        rowsum = sb("rowsum", [P, 4, 8])
        rinv = sb("rinv", [P, 4, 8])
        probsT = sb("probsT", [P, 2, 8, P])
        oT = sb("oT", [P, 2, 4, P])
        stats2 = sb("stats2", [P, 6])
        moments2 = sb("moments2", [P, 2])
        half_var2, square2, rstd2 = sb("half_var2", [P, 1]), sb("square2", [P, 1]), sb("rstd2", [P, 1])
        xn2T = sb("xn2T", [P, B * P])
        xn2T_hi, xn2T_lo = sb("xn2T_hi", [P, B * P], F32R), sb("xn2T_lo", [P, B * P], F32R)
        gu_raw = [sb(f"gu_raw{i}", [P, 2 * I_FFN]) for i in range(2)]
        gu_hi = [sb(f"gu_hi{i}", [P, 2 * I_FFN], F32R) for i in range(2)]
        gu_lo = [sb(f"gu_lo{i}", [P, 2 * I_FFN], F32R) for i in range(2)]
        down_sb = [sb(f"down{i}", [P, 2, P]) for i in range(2)]
        silu_sb = sb("silu_sb", [P, 2, 512])
        h_sb = sb("h_sb", [P, 2, 2, 512])
        z, ez, den, prob = (sb(n, [P, B, E_ROUTED]) for n in ("z", "ez", "den", "prob"))
        cand, hot1, hot2, prob2 = (sb(n, [P, B, E_ROUTED]) for n in ("cand", "hot1", "hot2", "prob2"))
        top1, top2, first, total = (sb(n, [P, B]) for n in ("top1", "top2", "first", "total"))
        w_all = sb("w_all", [P, EXPERTS, B])
        w_col = [sb(f"w_col{i}", [P, B]) for i in range(2)]

        s_bank = [bank("s_even"), bank("s_odd")]
        pt_bank = [bank("pt0"), bank("pt1")]
        proj_bank = {"q": bank("proj_q"), "k": bank("proj_k")}
        o_bank = bank("o_bank")
        misc = bank("misc")
        g_bank, u_bank = [s_bank[0], pt_bank[0]], [s_bank[1], pt_bank[1]]
        d_bank = [proj_bank["q"], proj_bank["k"]]
        last_bank = [misc, o_bank]

        in_x0, in_x, in_ctx0, in_ctx = sem("in_x0"), sem("in_x"), sem("in_ctx0"), sem("in_ctx")
        in_w = {n: [sem(f"in_w{n}0"), sem(f"in_w{n}1")] for n in "qkv"}
        in_wo, in_ident, in_rows, in_router = sem("in_wo"), sem("in_ident"), sem("in_rows"), sem("in_router")
        in_mask = [sem("in_mask0"), sem("in_mask1")]
        in_gu = [sem("in_gu0"), sem("in_gu1")]
        in_down = [sem("in_down0"), sem("in_down1")]
        out_sem = sem("out_sem")
        tanh_ready = sem("tanh_ready")
        whi_ready = {n: sem(f"w{n}hi_ready") for n in "qkv"}
        wlo_ready = {n: [sem(f"w{n}lo_ready{i}") for i in range(2)] for n in "qkv"}
        ckhi_ready, cklo_ready = sem("ckhi_ready"), sem("cklo_ready")
        ckhi_rest, cklo_rest = sem("ckhi_rest"), sem("cklo_rest")
        ln1_step, ln2_step = sem("ln1_step"), sem("ln2_step")
        xn_ready = sem("xn_ready")
        xn2_ready = sem("xn2_ready")
        xthi_ready = sem("xthi_ready")
        cvhi_ready, cvlo_ready = sem("cvhi_ready"), sem("cvlo_ready")
        misc_done, misc_free = sem("misc_done"), sem("misc_free")
        warm_ready = sem("warm_ready")
        q_done, q_free = sem("q_done"), sem("q_free")
        k_done, k_free = sem("k_done"), sem("k_free")
        s_done, ttr_done = sem("s_done"), sem("ttr_done")
        exp_done, rinv_ready, norm_done = sem("exp_done"), sem("rinv_ready"), sem("norm_done")
        t_done = sem("t_done")
        pt0_free, pt1_free = sem("pt0_free"), sem("pt1_free")
        o_done, ot_ready = sem("o_done"), sem("ot_ready")
        xn2t_ready, xn2hi_ready = sem("xn2t_ready"), sem("xn2hi_ready")
        carrier_ready = sem("carrier_ready")
        guhi_ready, gulo_ready = sem("guhi_ready"), sem("gulo_ready")
        gu_done, silu_done, h_done = sem("gu_done"), sem("silu_done"), sem("h_done")
        d_done, acc_done = sem("d_done"), sem("acc_done")
        d_last, acc_last = sem("d_last"), sem("acc_last")
        wcol_ready = sem("wcol_ready")
        r_done, z_ready, ez_ready = sem("r_done"), sem("z_ready"), sem("ez_ready")
        route_step, shared_ready = sem("route_step"), sem("shared_ready")

        block = stack.enter_context(nc.Block())

        @block.sync
        def _(sp):
            def load_w(name, src, half):
                cols = slice(half * 512, (half + 1) * 512)
                sp.dma_start(w_raw[name][:, cols], src[:, cols]).then_inc(in_w[name][half], 16)

            sp.dma_start(x_sb[:, 0:2, :], x[:, 0:2, :]).then_inc(in_x0, 16)
            load_w("k", wkT, 0)
            sp.dma_start(ctx_sb[:, 0:2 * P], ctxT[:, 0:2 * P]).then_inc(in_ctx0, 16)
            load_w("k", wkT, 1)
            load_w("q", wqT, 0)
            load_w("q", wqT, 1)
            sp.dma_start(x_sb[:, 2:B, :], x[:, 2:B, :]).then_inc(in_x, 16)
            sp.dma_start(mask_sb[0][:], mask[0]).then_inc(in_mask[0], 16)
            load_w("v", wvT, 0)
            load_w("v", wvT, 1)
            sp.dma_start(ctx_sb[:, 2 * P:], ctxT[:, 2 * P:]).then_inc(in_ctx, 16)
            sp.dma_start(mask_sb[1][:], mask[1]).then_inc(in_mask[1], 16)
            sp.dma_start(wo_sb[:], woT).then_inc(in_wo, 16)
            sp.dma_start(router_sb[:], routerT).then_inc(in_router, 16)
            for e in range(2):
                sp.dma_start(gu_raw[e][:], gu[e]).then_inc(in_gu[e], 16)
                sp.dma_start(down_sb[e][:], down[e]).then_inc(in_down[e], 16)
            with sp.Fori(1, PAIRS) as p:
                for i in range(2):
                    sp.wait_ge(ttr_done, HEADS * (2 * p + i - 1))
                    sp.dma_start(mask_sb[i][:], mask[bass.ds(2 * p + i, 1)].rearrange("o q k -> (o q) k")).then_inc(in_mask[i], 16)

            def load_expert(e, i, steps):
                sp.wait_ge(gulo_ready, e - 1)
                sp.dma_start(gu_raw[i][:], gu[bass.ds(e, 1)].rearrange("o h i -> (o h) i")).then_inc(in_gu[i], 16)
                sp.wait_ge(d_done, steps)
                sp.dma_start(down_sb[i][:], down[bass.ds(e, 1)].rearrange("o i c h -> (o i) c h")).then_inc(in_down[i], 16)

            load_expert(2, 0, 3)
            load_expert(3, 1, 4)
            with sp.Fori(2, EXPERTS // 2) as q:
                load_expert(2 * q, 0, 4 * q - 2)
                load_expert(2 * q + 1, 1, 4 * q)
            load_expert(EXPERTS - 1, 0, STEPS - 4)
            sp.wait_ge(acc_done, STEPS - 1)
            sp.dma_start(out[:, 0:B // 2, :], x_sb[:, 0:B // 2, :]).then_inc(out_sem, 16)
            for n, tiles in ((1, slice(B // 2, B // 2 + 2)), (2, slice(B // 2 + 2, B))):
                sp.wait_ge(acc_last, n)
                sp.dma_start(out[:, tiles, :], x_sb[:, tiles, :]).then_inc(out_sem, 16)
            sp.wait_ge(out_sem, 48)

        @block.tensor
        def _(pe):
            def three_pass(dst, a_hi, a_lo, b_hi, b_lo):
                pe.matmul(dst, a_hi, b_hi, start=True, stop=False)
                pe.matmul(dst, a_lo, b_hi, start=False, stop=False)
                return pe.matmul(dst, a_hi, b_lo, start=False, stop=True)

            def xn_transposes(batches, bank):
                for i, b in enumerate(batches):
                    mm = pe.transpose(bank[:, i * P:(i + 1) * P], xn[:, b, :], ident_sb[:])
                mm.then_inc(misc_done, 1)

            def project_unit(name, cols, u, at, done):
                hi, lo = (xT_hi, xT_lo) if name == "q" else (ck_hi, ck_lo)
                for c in (2 * u, 2 * u + 1):
                    w = slice(c * P, (c + 1) * P)
                    mm = three_pass(at[:, (c % 2) * 2 * P:(c % 2 + 1) * 2 * P], w_hi[name][:, w], w_lo[name][:, w],
                                    hi[:, cols], lo[:, cols])
                mm.then_inc(done, 1)

            def project(pair, u, name):
                free, done = (q_free, q_done) if name == "q" else (k_free, k_done)
                pe.wait_ge(free, PROJ_USES * pair + u)
                project_unit(name, bass.ds(pair * 2 * P, 2 * P), u, proj_bank[name], done)

            def project_v(pair, i):
                tok = slice(i * P, (i + 1) * P)
                pe.wait_ge(cvlo_ready, pair + 1)
                for half, (name, free, done) in enumerate((("q", q_free, q_done), ("k", k_free, k_done))):
                    pe.wait_ge(free, PROJ_USES * pair + 4 + i)
                    cols = slice(half * 512, (half + 1) * 512)
                    three_pass(proj_bank[name][:], cv_hi[:, tok], cv_lo[:, tok], w_hi["v"][:, cols],
                               w_lo["v"][:, cols]).then_inc(done, 1)

            def scores(g, pair, r, units=None):
                i, half = r // 2, r % 2
                q_units, k_units = units or (2 * half + 2, 2 * half + 2)
                pe.wait_ge(q_free, PROJ_USES * pair + q_units)
                pe.wait_ge(k_free, PROJ_USES * pair + k_units)
                if not (isinstance(g, int) and g == 0):
                    pe.wait_ge(ttr_done, 8 * g)
                for j in range(4):
                    for odd in range(2):
                        rows = slice(DK * odd, DK * (odd + 1))
                        mm = pe.matmul(s_bank[odd][:, j * P:(j + 1) * P], qT[rows, 4 * half + j, i * P:(i + 1) * P],
                                       kT[rows, 4 * half + j, i * P:(i + 1) * P], start=True, stop=True)
                mm.then_inc(s_done, 1)

            def transposes(g, r):
                for u, free in enumerate((pt0_free, pt1_free)):
                    pe.wait_ge(norm_done, 2 * g + u + 1)
                    if not (isinstance(g, int) and g == 0):
                        pe.wait_ge(free, g)
                    for j in range(4):
                        mm = pe.transpose(pt_bank[u][:, j * P:(j + 1) * P], probs[:, r, 4 * u + j, :], ident_sb[:])
                    mm.then_inc(t_done, 1)

            def values(g, pair, r):
                i, half = r // 2, r % 2
                pe.wait_ge(q_free, PROJ_USES * pair + 5 + i)
                pe.wait_ge(k_free, PROJ_USES * pair + 5 + i)
                pe.wait_ge(pt0_free, g + 1)
                pe.wait_ge(pt1_free, g + 1)
                if not (isinstance(g, int) and g == 0):
                    pe.wait_ge(ot_ready, g)
                for j in range(4):
                    for odd in range(2):
                        h = 8 * half + 2 * j + odd
                        mm = pe.matmul(o_bank[DK * odd:DK * (odd + 1), j * P:(j + 1) * P],
                                       v_sb[i][:, h * DK:(h + 1) * DK], probsT[:, half, 2 * j + odd, :],
                                       start=True, stop=True)
                mm.then_inc(o_done, 1)

            def out_project(b, use):
                pe.wait_ge(ot_ready, 2 * b + 2)
                pe.wait_ge(misc_free, use)
                for c in range(CHUNKS):
                    mm = pe.matmul(misc[:, 0:P], oT[:, c // 4, c % 4, :], wo_sb[:, c, :],
                                   start=(c == 0), stop=(c == CHUNKS - 1))
                mm.then_inc(misc_done, 1)

            pe.wait_ge(warm_ready, 1)
            for _ in range(WARM_UP):
                pe.matmul(misc[:, 0:P], warm[:], warm[:], start=True, stop=True)
            first = slice(0, 2 * P)
            pe.wait_ge(cklo_ready, 1)
            pe.wait_ge(wlo_ready["k"][0], 1)
            project_unit("k", first, 0, proj_bank["q"], q_done)
            pe.wait_ge(in_ident, 16)
            pe.wait_ge(xn_ready, 2)
            xn_transposes(range(2), misc)
            project_unit("k", first, 1, proj_bank["k"], k_done)
            pe.wait_ge(wlo_ready["q"][0], 1)
            pe.wait_ge(misc_free, 1)
            pe.wait_ge(q_free, 1)
            project_unit("q", first, 0, proj_bank["q"], q_done)
            pe.wait_ge(k_free, 1)
            project_unit("q", first, 1, proj_bank["k"], k_done)
            pe.wait_ge(wlo_ready["k"][1], 1)
            pe.wait_ge(q_free, 2)
            project_unit("k", first, 2, proj_bank["q"], q_done)
            pe.wait_ge(k_free, 2)
            project_unit("k", first, 3, proj_bank["k"], k_done)
            scores(0, 0, 0, units=(2, 2))
            pe.wait_ge(wlo_ready["q"][1], 1)
            pe.wait_ge(q_free, 3)
            project_unit("q", first, 2, proj_bank["q"], q_done)
            pe.wait_ge(k_free, 3)
            project_unit("q", first, 3, proj_bank["k"], k_done)
            pe.wait_ge(wlo_ready["v"][0], 1)
            pe.wait_ge(wlo_ready["v"][1], 1)
            project_v(0, 0)
            scores(1, 0, 1, units=(4, 4))
            project_v(0, 1)
            transposes(0, 0)
            scores(2, 0, 2)
            pe.wait_ge(xn_ready, B)
            xn_transposes(range(2, 6), misc)
            pe.wait_ge(q_free, PROJ_USES)
            xn_transposes(range(6, B), proj_bank["q"])
            values(0, 0, 0)
            pe.wait_ge(in_wo, 16)
            pe.wait_ge(cklo_rest, 1)

            with pe.Fori(0, PAIRS - 1) as p:
                g = 4 * p
                use = XT_USES + 1 + 2 * p
                transposes(g + 1, 1)
                scores(g + 3, p, 3)
                pe.wait_ge(misc_free, XT_USES + 1)
                project(p + 1, 0, "q")
                project(p + 1, 0, "k")
                values(g + 1, p, 1)
                project(p + 1, 1, "q")
                project(p + 1, 1, "k")
                transposes(g + 2, 2)
                out_project(2 * p, use)
                scores(g + 4, p + 1, 0)
                project(p + 1, 2, "q")
                project(p + 1, 2, "k")
                values(g + 2, p, 2)
                project(p + 1, 3, "k")
                project(p + 1, 3, "q")
                transposes(g + 3, 3)
                scores(g + 5, p + 1, 1)
                project_v(p + 1, 0)
                values(g + 3, p, 3)
                transposes(g + 4, 0)
                out_project(2 * p + 1, use + 1)
                scores(g + 6, p + 1, 2)
                project_v(p + 1, 1)
                values(g + 4, p + 1, 0)

            def gate_up(n, i, half, c):
                tok = slice(half * 512, (half + 1) * 512)
                for dst, at in ((g_bank[c], c * P), (u_bank[c], I_FFN + c * P)):
                    mm = three_pass(dst[:], gu_hi[i][:, at:at + P], gu_lo[i][:, at:at + P], xn2T_hi[:, tok], xn2T_lo[:, tok])
                mm.then_inc(gu_done, 1)

            def down_tile(dst, i, slot, t):
                for c in range(2):
                    mm = pe.matmul(dst, h_sb[:, slot, c, t * P:(t + 1) * P], down_sb[i][:, c, :], start=(c == 0), stop=(c == 1))
                return mm

            def down_step(j, i, slot):
                pe.wait_ge(h_done, 2 * j + 2)
                if not (isinstance(j, int) and j < 2):
                    pe.wait_ge(acc_done, j - 1)
                for t in range(4):
                    mm = down_tile(d_bank[slot][:, t * P:(t + 1) * P], i, slot, t)
                mm.then_inc(d_done, 1)

            last = PAIRS - 1
            use = XT_USES + B - 1
            transposes(13, 1)
            pe.wait_ge(xn2_ready, 4)
            pe.wait_ge(q_free, PROJ_USES * PAIRS)
            xn_transposes(range(4), proj_bank["q"])
            scores(15, last, 3)
            values(13, last, 1)
            transposes(14, 2)
            out_project(B - 2, use)
            values(14, last, 2)
            transposes(15, 3)
            pe.wait_ge(gulo_ready, 1)
            pe.wait_ge(misc_free, use + 1)
            pe.wait_ge(ttr_done, 8 * GROUPS)
            gate_up(0, 0, 0, 0)
            values(15, last, 3)
            pe.wait_ge(xn2_ready, 6)
            pe.wait_ge(k_free, PROJ_USES * PAIRS)
            xn_transposes(range(4, 6), proj_bank["k"])
            gate_up(1, 0, 0, 1)
            out_project(B - 1, use + 2)
            pe.wait_ge(in_down[0], 16)
            down_step(0, 0, 0)
            pe.wait_ge(gulo_ready, 2)
            pe.wait_ge(h_done, 1)
            gate_up(2, 1, 0, 0)
            pe.wait_ge(xn2_ready, B)
            pe.wait_ge(misc_free, use + 4)
            xn_transposes(range(6, B), misc)
            pe.wait_ge(h_done, 2)
            gate_up(3, 1, 0, 1)
            pe.wait_ge(misc_free, use + 5)
            pe.wait_ge(h_done, 3)
            gate_up(4, 0, 1, 0)
            pe.wait_ge(in_router, 16)
            pe.wait_ge(xn2t_ready, 3)
            for t in range(B):
                mm = pe.matmul(o_bank[:, t * E_ROUTED:(t + 1) * E_ROUTED], xn2T[:, t * P:(t + 1) * P], router_sb[:],
                               start=True, stop=True)
            mm.then_inc(r_done, 1)
            pe.wait_ge(h_done, 4)
            gate_up(5, 0, 1, 1)
            pe.wait_ge(in_down[1], 16)
            down_step(1, 1, 1)
            pe.wait_ge(h_done, 5)
            gate_up(6, 1, 1, 0)
            pe.wait_ge(h_done, 6)
            gate_up(7, 1, 1, 1)
            down_step(2, 0, 0)

            def expert_steps(e, i, loads):
                pe.wait_ge(gulo_ready, e + 1)
                for half in range(2):
                    j = 2 * e + half
                    for c in range(2):
                        pe.wait_ge(h_done, 2 * j + c - 1)
                        gate_up(2 * j + c, i, half, c)
                    if half == 1:
                        pe.wait_ge(in_down[i], 16 * loads)
                    down_step(j - 1, i if half else 1 - i, 1 - half)

            expert_steps(2, 0, 2)
            with pe.Fori(1, E_ROUTED // 2) as q:
                expert_steps(2 * q + 1, 1, q + 1)
                expert_steps(2 * q + 2, 0, q + 2)
            pe.wait_ge(h_done, 2 * STEPS)
            for t in range(4):
                mm = down_tile(last_bank[t // 2][:, (t % 2) * P:(t % 2 + 1) * P], 0, 1, t)
                if t % 2:
                    mm.then_inc(d_last, 1)

        @block.scalar
        def _(act):
            act.wait_ge(warm_ready, 1)
            act.activation(act_scratch[:], warm[:, 0:1], ACT.Exp)

            def split_hi(name, half):
                act.wait_ge(in_w[name][half], 16)
                cols = slice(half * 512, (half + 1) * 512)
                act.copy(w_hi[name][:, cols], w_raw[name][:, cols]).then_inc(whi_ready[name], 1)

            def xT_hi_part(n, batches, bank):
                act.wait_ge(misc_done, n)
                act.copy(xT_hi[:, batches[0] * P:(batches[-1] + 1) * P], bank[:, 0:len(batches) * P]).then_inc(xthi_ready, 1)

            def copy_q(pair, u):
                act.wait_ge(q_done, PROJ_USES * pair + u + 1)
                act.copy(qT[:, 2 * u:2 * u + 2, :].rearrange("p c t -> p (c t)"), proj_bank["q"][:]).then_inc(q_free, 1)

            def copy_v(pair, i):
                act.wait_ge(q_done, PROJ_USES * pair + 5 + i)
                act.copy(v_sb[i][:, 0:512], proj_bank["q"][:]).then_inc(q_free, 1)

            def exps(g, r, u):
                for l in range(4 * u, 4 * u + 4):
                    act.wait_ge(ttr_done, 8 * g + l + 1)
                    e = act.activation(probs[:, r, l, :], probs[:, r, l, :], ACT.Exp, bias=negmax[:, r, l:l + 1],
                                       scale=-1.0, accum_out=rowsum[:, r, l:l + 1])
                e.then_inc(exp_done, 1)

            def copy_pt(g, r):
                act.wait_ge(t_done, 2 * g + 1)
                act.copy(probsT[:, r % 2, 0:4, :].rearrange("p h q -> p (h q)"), pt_bank[0][:]).then_inc(pt0_free, 1)

            def xn2T_hi_part(batches, n, bank):
                act.wait_ge(misc_done, n)
                cols, width = slice(batches[0] * P, (batches[-1] + 1) * P), len(batches) * P
                act.copy(xn2T_hi[:, cols], bank[:, 0:width]).then_inc(xn2hi_ready, 1)

            split_hi("k", 0)
            act.wait_ge(in_ctx0, 16)
            act.copy(ck_hi[:, 0:2 * P], ctx_sb[:, 0:2 * P]).then_inc(ckhi_ready, 1)
            split_hi("k", 1)
            split_hi("q", 0)

            def copy_first(dst, u, n):
                act.wait_ge(q_done, n)
                act.copy(dst[:, 2 * u:2 * u + 2, :].rearrange("p c t -> p (c t)"), proj_bank["q"][:]).then_inc(q_free, 1)

            xT_hi_part(1, range(2), misc)
            copy_first(kT, 0, 1)
            split_hi("q", 1)
            copy_first(qT, 0, 2)
            split_hi("v", 0)
            copy_first(kT, 2, 3)
            split_hi("v", 1)
            act.wait_ge(in_rows, 16)
            act.activation(tanh_g[:], gates, ACT.Tanh).then_inc(tanh_ready, 1)
            copy_first(qT, 2, 4)
            exps(0, 0, 0)
            exps(0, 0, 1)
            copy_v(0, 0)
            exps(1, 1, 0)
            copy_pt(0, 0)
            copy_v(0, 1)
            exps(1, 1, 1)
            xT_hi_part(2, range(2, 6), misc)
            xT_hi_part(3, range(6, B), proj_bank["q"])
            exps(2, 2, 0)
            exps(2, 2, 1)

            with act.Fori(0, PAIRS - 1) as p:
                g = 4 * p
                use = XT_USES + 1 + 2 * p
                copy_pt(g + 1, 1)
                copy_q(p + 1, 0)
                exps(g + 3, 3, 0)
                copy_q(p + 1, 1)
                exps(g + 3, 3, 1)
                copy_pt(g + 2, 2)
                copy_q(p + 1, 2)
                exps(g + 4, 0, 0)
                copy_q(p + 1, 3)
                exps(g + 4, 0, 1)
                copy_pt(g + 3, 3)
                exps(g + 5, 1, 0)
                copy_v(p + 1, 0)
                exps(g + 5, 1, 1)
                copy_pt(g + 4, 0)
                exps(g + 6, 2, 0)
                copy_v(p + 1, 1)
                exps(g + 6, 2, 1)

            def silu(n, c):
                act.wait_ge(gu_done, n + 1)
                act.activation(silu_sb[:, c, :], g_bank[c][:], ACT.Silu).then_inc(silu_done, 1)

            use = XT_USES + B - 1
            copy_pt(13, 1)
            xn2T_hi_part(range(4), use + 1, proj_bank["q"])
            exps(15, 3, 0)
            exps(15, 3, 1)
            copy_pt(14, 2)
            copy_pt(15, 3)
            silu(0, 0)
            xn2T_hi_part(range(4, 6), use + 3, proj_bank["k"])
            silu(1, 1)
            silu(2, 0)
            xn2T_hi_part(range(6, B), use + 5, misc)
            silu(3, 1)
            silu(4, 0)
            act.wait_ge(z_ready, 1)
            act.activation(ez[:], z[:], ACT.Exp, scale=-1.0).then_inc(ez_ready, 1)
            for n in range(5, 12):
                silu(n, n % 2)
            with act.Fori(1, E_ROUTED // 2) as q:
                for s in range(4):
                    for c in range(2):
                        silu(8 * q + 4 + 2 * s + c, c)

        @block.vector
        def _(dve):
            def carry_wait(column):
                dve.memset(carrier[:, column:column + 1], 0.0)

            def norm1_steps(tiles, n):
                a, b = tiles[0], tiles[-1] + 1
                var, sq, y = half_var[:, a:b], square[:, a:b], rstd[:, a:b]
                for t in tiles:
                    dve.bn_stats(stats[:, t, :], x_sb[:, t, :]).then_inc(ln1_step, 1)
                    yield
                n += b - a
                dve.wait_ge(ln1_step, n)
                for t in tiles:
                    dve.bn_aggr(moments[:, t, :], stats[:, t, :]).then_inc(ln1_step, 1)
                yield
                n += b - a
                dve.wait_ge(ln1_step, n)
                dve.tensor_scalar(var, moments[:, a:b, 1], EPS, -0.5, ALU.add, ALU.mult).then_inc(ln1_step, 1)
                yield
                dve.wait_ge(ln1_step, n + 1)
                dve.tensor_scalar(y.bitcast(I32), var.bitcast(I32), -0.5, SEED, ALU.mult, ALU.add).then_inc(ln1_step, 1)
                yield
                n += 2
                for _ in range(NEWTON):
                    dve.wait_ge(ln1_step, n)
                    dve.tensor_tensor(sq, y, y, ALU.mult).then_inc(ln1_step, 1)
                    yield
                    dve.wait_ge(ln1_step, n + 1)
                    dve.tensor_tensor(sq, sq, var, ALU.mult).then_inc(ln1_step, 1)
                    yield
                    dve.wait_ge(ln1_step, n + 2)
                    dve.scalar_tensor_tensor(y, sq, 1.5, y, ALU.add, ALU.mult).then_inc(ln1_step, 1)
                    yield
                    n += 3
                dve.wait_ge(ln1_step, n)
                for t in tiles:
                    dve.tensor_scalar(xn[:, t, :], x_sb[:, t, :], moments[:, t, 0:1], rstd[:, t:t + 1],
                                      ALU.subtract, ALU.mult).then_inc(xn_ready, 1)
                    yield

            def split_lo(name, half):
                dve.wait_ge(whi_ready[name], half + 1)
                cols = slice(half * 512, (half + 1) * 512)
                dve.tensor_tensor(w_lo[name][:, cols], w_raw[name][:, cols], w_hi[name][:, cols].bitcast(F32),
                                  ALU.subtract).then_inc(wlo_ready[name][half], 1)

            def xT_lo_part(n, batches, bank):
                dve.wait_ge(xthi_ready, n)
                cols = slice(batches[0] * P, (batches[-1] + 1) * P)
                dve.tensor_tensor(xT_lo[:, cols], bank[:, 0:len(batches) * P], xT_hi[:, cols].bitcast(F32),
                                  ALU.subtract).then_inc(misc_free, 1)

            def copy_k(pair, u):
                dve.wait_ge(k_done, PROJ_USES * pair + u + 1)
                dve.tensor_copy(kT[:, 2 * u:2 * u + 2, :].rearrange("p c t -> p (c t)"), proj_bank["k"][:]).then_inc(k_free, 1)

            def copy_v(pair, i):
                dve.wait_ge(k_done, PROJ_USES * pair + 5 + i)
                dve.tensor_copy(v_sb[i][:, 512:], proj_bank["k"][:]).then_inc(k_free, 1)

            def mask_max(g, b2, r, between=iter(())):
                dve.wait_ge(s_done, g + 1)
                dve.wait_ge(in_mask[r // 2], 16 * (b2 + 1))
                carry_wait(0)
                for l in range(8):
                    dve.tensor_tensor_reduce(probs[:, r, l, :], s_bank[l % 2][:, (l // 2) * P:(l // 2 + 1) * P],
                                             mask_sb[r // 2][:], -1.0, HUGE, ALU.add, ALU.min,
                                             negmax[:, r, l:l + 1]).then_inc(ttr_done, 1)
                    next(between, None)

            def after(heads, step, *args):
                for _ in range(heads - 1):
                    yield
                step(*args)

            def recips(g, r, quads=(0, 1)):
                for u in quads:
                    dve.wait_ge(exp_done, 2 * g + u + 1)
                    dve.reciprocal(rinv[:, r, 4 * u:4 * u + 4], rowsum[:, r, 4 * u:4 * u + 4]).then_inc(rinv_ready, 1)

            def copy_pt(g, r):
                dve.wait_ge(t_done, 2 * g + 2)
                dve.tensor_copy(probsT[:, r % 2, 4:8, :].rearrange("p h q -> p (h q)"), pt_bank[1][:]).then_inc(pt1_free, 1)

            def copy_o(g, r):
                dve.wait_ge(o_done, g + 1)
                dve.tensor_copy(oT[:, r % 2, :, :].rearrange("p c q -> p (c q)"), o_bank[:]).then_inc(ot_ready, 1)

            def x_of(b):
                return x_sb[:, bass.ds(b, 1), :].rearrange("p o d -> p (o d)")

            def add_attention(b, use):
                dve.wait_ge(misc_done, use + 1)
                dve.scalar_tensor_tensor(x_of(b), misc[:, 0:P], tanh_g[:, 0:1], x_of(b), ALU.mult, ALU.add).then_inc(misc_free, 1)

            def norm2_steps(b, use):
                n = LN2_STEPS * b
                dve.wait_ge(misc_free, use + 1)
                carry_wait(1)
                dve.bn_stats(stats2[:], x_of(b)).then_inc(ln2_step, 1)
                yield
                dve.wait_ge(ln2_step, n + 1)
                carry_wait(1)
                dve.bn_aggr(moments2[:], stats2[:]).then_inc(ln2_step, 1)
                yield
                dve.wait_ge(ln2_step, n + 2)
                dve.tensor_scalar(half_var2[:], moments2[:, 1:2], EPS, -0.5, ALU.add, ALU.mult).then_inc(ln2_step, 1)
                yield
                dve.wait_ge(ln2_step, n + 3)
                dve.tensor_scalar(rstd2[:].bitcast(I32), half_var2[:].bitcast(I32), -0.5, SEED, ALU.mult,
                                  ALU.add).then_inc(ln2_step, 1)
                yield
                for k in range(NEWTON):
                    dve.wait_ge(ln2_step, n + 4 + 2 * k)
                    dve.tensor_scalar(square2[:], rstd2[:], rstd2[:], half_var2[:], ALU.mult, ALU.mult).then_inc(ln2_step, 1)
                    yield
                    dve.wait_ge(ln2_step, n + 5 + 2 * k)
                    dve.scalar_tensor_tensor(rstd2[:], square2[:], 1.5, rstd2[:], ALU.add, ALU.mult).then_inc(ln2_step, 1)
                    yield
                dve.wait_ge(ln2_step, n + LN2_STEPS)
                xn_b = xn[:, bass.ds(b, 1), :].rearrange("p o d -> p (o d)")
                dve.tensor_scalar(xn_b, x_of(b), moments2[:, 0:1], rstd2[:], ALU.subtract, ALU.mult).then_inc(xn2_ready, 1)
                yield

            def run(steps, count):
                for _ in range(count):
                    next(steps, None)

            def finish(steps):
                for _ in steps:
                    pass

            def xn2T_lo_part(n, batches, bank):
                dve.wait_ge(xn2hi_ready, n)
                cols = slice(batches[0] * P, (batches[-1] + 1) * P)
                dve.tensor_tensor(xn2T_lo[:, cols], bank[:, 0:len(batches) * P], xn2T_hi[:, cols].bitcast(F32),
                                  ALU.subtract).then_inc(misc_free, 1)

            def copy_first(dst, u, n):
                dve.wait_ge(k_done, n)
                dve.tensor_copy(dst[:, 2 * u:2 * u + 2, :].rearrange("p c t -> p (c t)"), proj_bank["k"][:]).then_inc(k_free, 1)

            dve.memset(warm[:], 0.0).then_inc(warm_ready, 1)
            dve.wait_ge(in_x0, 16)
            steps = norm1_steps(range(2), 0)
            run(steps, 9)
            dve.wait_ge(in_ctx0, 16)
            dve.wait_ge(ckhi_ready, 1)
            dve.tensor_tensor(ck_lo[:, 0:2 * P], ctx_sb[:, 0:2 * P], ck_hi[:, 0:2 * P].bitcast(F32),
                              ALU.subtract).then_inc(cklo_ready, 1)
            finish(steps)
            xT_lo_part(1, range(2), misc)
            copy_first(kT, 1, 1)
            split_lo("q", 1)
            copy_first(qT, 1, 2)
            dve.wait_ge(in_x, 16)
            steps = norm1_steps(range(2, B), 4 + 2 + 3 * NEWTON)
            run(steps, 3)
            copy_first(kT, 3, 3)
            run(steps, 4)

            def among_first():
                yield from islice(steps, 3)
                copy_first(qT, 3, 4)
                yield
                yield from islice(steps, 4)

            mask_max(0, 0, 0, among_first())
            recips(0, 0, (0,))
            copy_v(0, 0)
            run(steps, 6)
            recips(0, 0, (1,))
            mask_max(1, 0, 1)
            finish(steps)
            recips(1, 1, (0,))
            copy_pt(0, 0)
            copy_v(0, 1)
            recips(1, 1, (1,))

            mask_max(2, 0, 2)
            xT_lo_part(2, range(2, 6), misc)
            xT_lo_part(3, range(6, B), proj_bank["q"])
            copy_o(0, 0)
            recips(2, 2)
            dve.wait_ge(tanh_ready, 1)

            with dve.Fori(0, PAIRS - 1) as p:
                g = 4 * p
                use = XT_USES + 1 + 2 * p
                copy_pt(g + 1, 1)
                mask_max(g + 3, p, 3, after(4, copy_k, p + 1, 0))
                copy_o(g + 1, 1)
                recips(g + 3, 3)
                copy_k(p + 1, 1)
                copy_pt(g + 2, 2)
                add_attention(2 * p, use)
                mask_max(g + 4, p + 1, 0, after(4, copy_k, p + 1, 2))
                copy_o(g + 2, 2)
                copy_k(p + 1, 3)
                recips(g + 4, 0)
                copy_pt(g + 3, 3)
                steps = norm2_steps(2 * p, use)
                mask_max(g + 5, p + 1, 1, islice(steps, 5))
                copy_o(g + 3, 3)
                run(steps, 1)
                copy_v(p + 1, 0)
                run(steps, 1)
                recips(g + 5, 1)
                finish(steps)
                copy_pt(g + 4, 0)
                add_attention(2 * p + 1, use + 1)
                steps = norm2_steps(2 * p + 1, use + 1)
                mask_max(g + 6, p + 1, 2, steps)
                copy_o(g + 4, 0)
                run(steps, 1)
                copy_v(p + 1, 1)
                run(steps, 1)
                recips(g + 6, 2)
                finish(steps)

            def hidden(n, slot, c):
                dve.wait_ge(silu_done, n + 1)
                dve.tensor_tensor(h_sb[:, slot, c, :], silu_sb[:, c, :], u_bank[c][:], ALU.mult).then_inc(h_done, 1)

            def column(e, i):
                dve.tensor_copy(w_col[i][:], w_all[:, bass.ds(e, 1), :].rearrange("p o t -> p (o t)")).then_inc(wcol_ready, 1)

            def add_expert(j, e, i, half, slot, before=None):
                dve.wait_ge(d_done, j + 1)
                dve.wait_ge(wcol_ready, e + 1)
                if before is not None:
                    dve.wait_ge(acc_done, before)
                for t in range(4):
                    tile = 4 * half + t
                    a = dve.scalar_tensor_tensor(x_sb[:, tile, :], d_bank[slot][:, t * P:(t + 1) * P],
                                                 w_col[i][:, tile:tile + 1], x_sb[:, tile, :], ALU.mult, ALU.add)
                a.then_inc(acc_done, 1)

            use = XT_USES + B - 1
            copy_pt(13, 1)
            mask_max(15, PAIRS - 1, 3, after(6, copy_o, 13, 1))
            recips(15, 3, (0,))
            copy_pt(14, 2)
            recips(15, 3, (1,))
            xn2T_lo_part(1, range(4), proj_bank["q"])
            add_attention(B - 2, use + 1)
            steps = norm2_steps(B - 2, use + 1)
            run(steps, 2)
            copy_o(14, 2)
            run(steps, 3)
            copy_pt(15, 3)
            finish(steps)
            dve.tensor_copy(w_all[:, 0, :], tanh_g[:, 1:2].to_broadcast([P, B])).then_inc(shared_ready, 1)
            copy_o(15, 3)
            hidden(0, 0, 0)
            dve.wait_ge(shared_ready, 1)
            column(0, 0)
            xn2T_lo_part(2, range(4, 6), proj_bank["k"])
            hidden(1, 0, 1)
            add_attention(B - 1, use + 3)
            steps = norm2_steps(B - 1, use + 3)
            finish(steps)
            hidden(2, 1, 0)
            xn2T_lo_part(3, range(6, B), misc)
            hidden(3, 1, 1)
            add_expert(0, 0, 0, 0, 0)
            hidden(4, 0, 0)
            dve.wait_ge(in_rows, 16)
            dve.wait_ge(r_done, 1)
            dve.tensor_tensor(z[:], o_bank[:, 0:B * E_ROUTED].rearrange("p (t e) -> p t e", t=B),
                              bias_sb.unsqueeze(1).to_broadcast([P, B, E_ROUTED]), ALU.add).then_inc(z_ready, 1)

            def tiles(a):
                return a[:].unsqueeze(2).to_broadcast([P, B, E_ROUTED])

            def routing_steps():
                done = [0]

                def chained(instruction):
                    done[0] += 1
                    instruction.then_inc(route_step, 1)
                    return done[0]

                def first_of(values, top, hot):
                    yield chained(dve.tensor_reduce(top[:], values[:], AX, ALU.max))
                    yield chained(dve.tensor_tensor(cand[:], values[:], tiles(top), ALU.is_equal))
                    yield chained(dve.tensor_tensor(cand[:], cand[:], iota_sb.unsqueeze(1).to_broadcast([P, B, E_ROUTED]), ALU.mult))
                    yield chained(dve.tensor_reduce(first[:], cand[:], AX, ALU.min))
                    yield chained(dve.tensor_tensor(hot[:], cand[:], tiles(first), ALU.is_equal))

                yield chained(dve.tensor_scalar(den[:], ez[:], 1.0, None, ALU.add))
                yield chained(dve.reciprocal(prob[:], den[:]))
                yield from first_of(prob, top1, hot1)
                yield chained(dve.scalar_tensor_tensor(prob2[:], hot1[:], -2.0, prob[:], ALU.mult, ALU.add))
                yield from first_of(prob2, top2, hot2)
                yield chained(dve.tensor_tensor(total[:], top1[:], top2[:], ALU.add))
                yield chained(dve.reciprocal(total[:], total[:]))
                yield chained(dve.tensor_scalar(total[:], total[:], tanh_g[:, 1:2], None, ALU.mult))
                yield chained(dve.tensor_tensor(hot1[:], hot1[:], tiles(top1), ALU.mult))
                yield chained(dve.tensor_tensor(hot2[:], hot2[:], tiles(top2), ALU.mult))
                yield chained(dve.tensor_tensor(hot1[:], hot1[:], hot2[:], ALU.add))
                yield chained(dve.tensor_tensor(w_all[:, 1:, :].rearrange("p e t -> p t e"), hot1[:], tiles(total), ALU.mult))

            ROUTING_STEPS = 20

            def run_routing(steps, count):
                for _ in range(count):
                    n = next(steps, None)
                    if n is not None:
                        dve.wait_ge(route_step, n)

            routing = routing_steps()
            dve.wait_ge(ez_ready, 1)
            run_routing(routing, 5)
            hidden(5, 0, 1)
            run_routing(routing, 8)
            hidden(6, 1, 0)
            run_routing(routing, 3)
            hidden(7, 1, 1)
            run_routing(routing, ROUTING_STEPS)
            column(1, 1)
            add_expert(1, 1, 1, 0, 1, before=1)
            hidden(8, 0, 0)
            add_expert(2, 0, 0, 1, 0)

            def expert_steps(e, i, chunks=(0, 1)):
                for c in chunks:
                    hidden(4 * e + c, 0, c)
                add_expert(2 * e - 1, e - 1, 1 - i, 1, 1, before=3 if isinstance(e, int) else 2 * e - 2)
                for c in range(2):
                    hidden(4 * e + 2 + c, 1, c)
                column(e, i)
                add_expert(2 * e, e, i, 0, 0, before=2 * e - 1)

            expert_steps(2, 0, chunks=(1,))
            with dve.Fori(1, E_ROUTED // 2) as q:
                expert_steps(2 * q + 1, 1)
                expert_steps(2 * q + 2, 0)
            dve.wait_ge(acc_done, STEPS - 2)
            for t in range(B // 2):
                tile = B // 2 + t
                if t % 2 == 0:
                    dve.wait_ge(d_last, t // 2 + 1)
                a = dve.scalar_tensor_tensor(x_sb[:, tile, :], last_bank[t // 2][:, (t % 2) * P:(t % 2 + 1) * P],
                                             w_col[0][:, tile:tile + 1], x_sb[:, tile, :], ALU.mult, ALU.add)
                if t % 2:
                    a.then_inc(acc_last, 1)

        @block.gpsimd
        def _(pool):
            pool.memset(carrier[:, 2:3], 0.0).then_inc(carrier_ready, 1)
            pool.wait_ge(carrier_ready, 1)

            def carry_wait():
                pool.tensor_tensor(carrier[:, 3:4], carrier[:, 2:3], carrier[:, 2:3], ALU.add)

            def split_ctx(pair):
                cols = bass.ds(pair * 2 * P, 2 * P)
                pool.tensor_copy(cv_hi[:], ctx_sb[:, cols]).then_inc(cvhi_ready, 1)
                pool.wait_ge(cvhi_ready, pair + 1)
                carry_wait()
                pool.tensor_tensor(cv_lo[:], ctx_sb[:, cols], cv_hi[:].bitcast(F32), ALU.subtract).then_inc(cvlo_ready, 1)

            def split_lo(name, half):
                pool.wait_ge(whi_ready[name], half + 1)
                cols = slice(half * 512, (half + 1) * 512)
                pool.tensor_tensor(w_lo[name][:, cols], w_raw[name][:, cols], w_hi[name][:, cols].bitcast(F32),
                                   ALU.subtract).then_inc(wlo_ready[name][half], 1)

            def normalise(g, r):
                for u in range(2):
                    quad = probs[:, r, 4 * u:4 * u + 4, :]
                    pool.wait_ge(rinv_ready, 2 * g + u + 1)
                    pool.tensor_tensor(quad, quad, rinv[:, r, 4 * u:4 * u + 4].unsqueeze(2).to_broadcast([P, 4, P]),
                                       ALU.mult).then_inc(norm_done, 1)

            def split_expert(e, i, n):
                pool.wait_ge(in_gu[i], 16 * n)
                carry_wait()
                pool.tensor_copy(gu_hi[i][:], gu_raw[i][:]).then_inc(guhi_ready, 1)
                pool.wait_ge(guhi_ready, e + 1)
                pool.tensor_tensor(gu_lo[i][:], gu_raw[i][:], gu_hi[i][:].bitcast(F32), ALU.subtract).then_inc(gulo_ready, 1)

            pool.dma_start(ident_sb[:], ident).then_inc(in_ident, 16)
            pool.dma_start(rows_sb[:], rows.partition_broadcast(P)).then_inc(in_rows, 16)
            split_lo("k", 0)
            split_lo("k", 1)
            split_lo("q", 0)
            pool.wait_ge(in_ctx0, 16)
            split_ctx(0)
            split_lo("v", 0)
            split_lo("v", 1)
            pool.wait_ge(in_ctx, 16)
            pool.tensor_copy(ck_hi[:, 2 * P:], ctx_sb[:, 2 * P:]).then_inc(ckhi_rest, 1)
            pool.wait_ge(ckhi_rest, 1)
            pool.tensor_tensor(ck_lo[:, 2 * P:], ctx_sb[:, 2 * P:], ck_hi[:, 2 * P:].bitcast(F32),
                               ALU.subtract).then_inc(cklo_rest, 1)
            normalise(0, 0)
            normalise(1, 1)
            split_expert(0, 0, 1)
            normalise(2, 2)
            split_expert(1, 1, 1)
            with pool.Fori(0, PAIRS - 1) as p:
                normalise(4 * p + 3, 3)
                pool.wait_ge(k_done, PROJ_USES * (p + 1))
                carry_wait()
                split_ctx(p + 1)
                for r in range(3):
                    normalise(4 * p + 4 + r, r)
            normalise(GROUPS - 1, 3)
            for n, batches in enumerate((range(4), range(4, 6), range(6, B))):
                pool.wait_ge(misc_free, XT_USES + B + 2 * n)
                cols = slice(batches[0] * P, (batches[-1] + 1) * P)
                pool.tensor_tensor(xn2T[:, cols], xn2T_hi[:, cols].bitcast(F32), xn2T_lo[:, cols].bitcast(F32),
                                   ALU.add).then_inc(xn2t_ready, 1)

            def next_expert(e, i, n, units):
                pool.wait_ge(gu_done, units)
                split_expert(e, i, n)

            next_expert(2, 0, 2, 6)
            next_expert(3, 1, 2, 8)
            with pool.Fori(2, EXPERTS // 2) as q:
                next_expert(2 * q, 0, q + 1, 8 * q - 4)
                next_expert(2 * q + 1, 1, q + 1, 8 * q)
            next_expert(EXPERTS - 1, 0, EXPERTS // 2 + 1, 2 * STEPS - 8)


def kernel(x, ctx_1024, fside_Bx1xSxS2_0, g_xattn, g_ffn, L0_xattn_Wq, L0_xattn_Wk, L0_xattn_Wv, L0_xattn_Wo,
           L0_ffn_shared_gate, L0_ffn_shared_up, L0_ffn_shared_down, L0_ffn_gate_w, L0_ffn_up_w, L0_ffn_down_w,
           L0_ffn_router_w, L0_ffn_routing_bias):
    import numpy as np
    import concourse.bacc as bacc
    from concourse.bass_utils import run_bass_kernel_spmd

    a = np.asarray
    wo = a(L0_xattn_Wo).T.reshape(CHUNKS, P, P).transpose(1, 0, 2)
    gate = np.concatenate([a(L0_ffn_shared_gate).T[None], a(L0_ffn_gate_w)])
    up = np.concatenate([a(L0_ffn_shared_up).T[None], a(L0_ffn_up_w)])
    down = np.concatenate([a(L0_ffn_shared_down).T[None], a(L0_ffn_down_w)])
    arrays = {
        "x": a(x).transpose(1, 0, 2),
        "ctxT": a(ctx_1024).transpose(2, 0, 1).reshape(P, B * P),
        "mask": a(fside_Bx1xSxS2_0).reshape(B, P, P),
        "wqT": a(L0_xattn_Wq).T,
        "wkT": a(L0_xattn_Wk).T,
        "wvT": a(L0_xattn_Wv).T,
        "woT": wo,
        "gu": np.concatenate([gate, up], axis=2),
        "down": down.reshape(EXPERTS, 2, P, P).transpose(0, 2, 1, 3),
        "routerT": a(L0_ffn_router_w).T,
        "rows": np.concatenate([a(g_xattn), a(g_ffn), a(L0_ffn_routing_bias), np.arange(-E_ROUTED, 0, dtype=np.float32)]),
        "ident": np.eye(P, dtype=np.float32),
    }
    arrays = {n: np.ascontiguousarray(v) for n, v in arrays.items()}
    nc = bacc.Bacc("TRN2", target_bir_lowering=False, num_devices=1)
    args = {n: nc.dram_tensor(n, v.shape, mybir.dt.from_np(v.dtype), kind="ExternalInput").ap() for n, v in arrays.items()}
    args["out"] = nc.dram_tensor("out", (P, B, P), F32, kind="ExternalOutput").ap()
    build(nc, **args)
    result = run_bass_kernel_spmd(nc, [arrays], core_ids=[0])
    return result.results[0]["out"].transpose(1, 0, 2)
```
